# Optimizing a Trainium2 kernel written in Bass

```python
import numpy as np
import jax
import jax.numpy as jnp

def _softmax(x, axis=-1):
    return jax.nn.softmax(x, axis=axis)

def _gelu(x):
    return jax.nn.gelu(x, approximate=True)

def _silu(x):
    return jax.nn.silu(x)

def _sigmoid(x):
    return jax.nn.sigmoid(x)

def _layernorm(x, axis=-1, eps=1e-05):
    m = jnp.mean(x, axis=axis, keepdims=True)
    v = jnp.var(x, axis=axis, keepdims=True)
    return (x - m) / jnp.sqrt(v + eps)

def _scatter_add(tgt, idx, src, axis=0):
    return tgt.at[idx].add(src)

def _segment_sum(src, seg, n):
    return jax.ops.segment_sum(src, seg, n)
kernel_name = 'mk_gnn_preln_d4_gnn_r8_7ad552'

def setup_inputs(seed: int=0):
    np.random.seed(seed)
    _w = jnp.asarray

    def _rec_inputs():
        import jax
        import jax.numpy as jnp
        _gk = jax.random.key(seed)
        x = -0.0001006 + 1 * jax.random.normal(jax.random.fold_in(_gk, 1), (12500, 48), jnp.float32)
        _s = jax.random.randint(jax.random.fold_in(_gk, 2), (100000,), 0, 12500, jnp.int32)
        _d = jax.random.randint(jax.random.fold_in(_gk, 3), (100000,), 0, 12500, jnp.int32)
        _loop = jnp.arange(12500, dtype=jnp.int32)
        src = jnp.concatenate([_s, _d, _loop])
        dst = jnp.concatenate([_d, _s, _loop])
        _o = jnp.argsort(dst, stable=True)
        src = src[_o]
        dst = dst[_o]
        edge_attr_40 = jax.random.uniform(jax.random.fold_in(_gk, 13), (212500, 40), jnp.float32, 0.0, 1)
        edge_weight = jax.random.uniform(jax.random.fold_in(_gk, 15), (212500,), jnp.float32, 0.0, 0.999999)
        edge_weight1 = -0.000414295 + 0.999828 * jax.random.normal(jax.random.fold_in(_gk, 16), (212500, 1), jnp.float32)
        node_type_119 = jax.random.randint(jax.random.fold_in(_gk, 17), (12500,), 0, 119, jnp.int32)
        node_vec = jax.random.uniform(jax.random.fold_in(_gk, 18), (12500,), jnp.float32, 0.0, 1.49999)
        return (x, src, dst, edge_attr_40, edge_weight, edge_weight1, node_type_119, node_vec)
    x, src, dst, edge_attr_40, edge_weight, edge_weight1, node_type_119, node_vec = _rec_inputs()

    def _L0_gnn_setup():
        import jax, jax.numpy as jnp
        import numpy as np
        NUM_NODES = 12500
        key = jax.random.key(seed)
        k1, k2, k3 = jax.random.split(key, 3)
        x = jax.random.normal(k1, (NUM_NODES, 48), dtype=jnp.float32)
        edge_index = jax.random.randint(k2, (2, 200000), 0, NUM_NODES, dtype=jnp.int64)
        edge_weight = jax.random.uniform(k3, (200000,), dtype=jnp.float32)
        return {'x': x, 'edge_index': edge_index, 'edge_weight': edge_weight}
    _L0_gnn_all = _L0_gnn_setup()
    _L0_gnn_in = {k: v for k, v in _L0_gnn_all.items() if k in ()}
    del _L0_gnn_all

    def _L1_gnn_setup():
        import jax, jax.numpy as jnp
        import numpy as np
        CUTOFF = 6.0
        LN_EPS = 1e-05
        key = jax.random.key(seed)
        ks = jax.random.split(key, 16)
        N, E, H, R, NEL, G = (6250, 100000, 48, 40, 119, 32)
        inp = {'h': jax.random.normal(ks[0], (N, H), jnp.float32), 'edge_index': jax.random.randint(ks[1], (2, E), 0, N, jnp.int64), 'edge_attr': jax.random.uniform(ks[2], (E, R), jnp.float32), 'distances': jax.random.uniform(ks[3], (E,), jnp.float32) * 7.0, 'atom_z': jax.random.randint(ks[4], (N,), 0, NEL, jnp.int64), 'node_mult': jax.random.uniform(ks[5], (N,), jnp.float32) + 0.5, 'batch': jnp.zeros((N,), jnp.int64), 'W1': jax.random.normal(ks[6], (H, R), jnp.float32) / np.sqrt(R), 'b1': jax.random.normal(ks[7], (H,), jnp.float32) * 0.01, 'W2': jax.random.normal(ks[8], (H, H), jnp.float32) / np.sqrt(H), 'b2': jax.random.normal(ks[9], (H,), jnp.float32) * 0.01, 'emb': jax.random.normal(ks[10], (NEL, G), jnp.float32) * 0.01, 'adaptW': jax.random.normal(ks[11], (G, G), jnp.float32) * 0.01, 'gamma': jnp.ones((H,), jnp.float32), 'beta': jnp.zeros((H,), jnp.float32)}
        return inp
    _L1_gnn_all = _L1_gnn_setup()
    _L1_gnn_in = {k: v for k, v in _L1_gnn_all.items() if k in ('W1', 'b1', 'W2', 'b2', 'emb', 'adaptW', 'gamma', 'beta')}
    del _L1_gnn_all

    def _L2_gnn_setup():
        import jax, jax.numpy as jnp
        import numpy as np
        N_NODES = 12500
        N_EDGES = 200000
        N_CLASSES = 48
        key = jax.random.key(seed)
        k1, k2, k3, k4 = jax.random.split(key, 4)
        soft_label = jax.random.normal(k1, (N_NODES, N_CLASSES), dtype=jnp.float32)
        e = jax.random.normal(k2, (N_EDGES, 1), dtype=jnp.float32)
        src = jax.random.randint(k3, (N_EDGES,), 0, N_NODES)
        dst = jax.random.randint(k4, (N_EDGES,), 0, N_NODES)
        return {'soft_label': soft_label, 'e': e, 'src': src, 'dst': dst}
    _L2_gnn_all = _L2_gnn_setup()
    _L2_gnn_in = {k: v for k, v in _L2_gnn_all.items() if k in ()}
    del _L2_gnn_all

    def _L3_gnn_setup():
        import jax, jax.numpy as jnp
        import numpy as np
        NUM_LAYERS = 2
        N_NODES = 12500
        N_EDGES = 200000
        D_FEAT = 48

        def spmm(edge_index, edge_weight, x, n):
            src, dst = (edge_index[0], edge_index[1])
            msgs = x[src] * edge_weight[:, None]
            return jax.ops.segment_sum(msgs, dst, num_segments=n)
        key = jax.random.key(seed)
        k1, k2, k3 = jax.random.split(key, 3)
        features = jax.random.normal(k1, (N_NODES, D_FEAT), dtype=jnp.float32)
        edge_weight = jax.random.uniform(k2, (N_EDGES,), dtype=jnp.float32)
        edge_index = jax.random.randint(k3, (2, N_EDGES), 0, N_NODES, dtype=jnp.int64)
        return {'features': features, 'edge_weight': edge_weight, 'edge_index': edge_index}
    _L3_gnn_all = _L3_gnn_setup()
    _L3_gnn_in = {k: v for k, v in _L3_gnn_all.items() if k in ()}
    del _L3_gnn_all
    return {'x': x, 'src': src, 'dst': dst, 'edge_attr_40': edge_attr_40, 'edge_weight': edge_weight, 'edge_weight1': edge_weight1, 'node_type_119': node_type_119, 'node_vec': node_vec, 'L1_gnn_W1': _L1_gnn_in['W1'], 'L1_gnn_b1': _L1_gnn_in['b1'], 'L1_gnn_W2': _L1_gnn_in['W2'], 'L1_gnn_b2': _L1_gnn_in['b2'], 'L1_gnn_emb': _L1_gnn_in['emb'], 'L1_gnn_adaptW': _L1_gnn_in['adaptW'], 'L1_gnn_gamma': _L1_gnn_in['gamma'], 'L1_gnn_beta': _L1_gnn_in['beta']}

def reference(x, src, dst, edge_attr_40, edge_weight, edge_weight1, node_type_119, node_vec, L1_gnn_W1, L1_gnn_b1, L1_gnn_W2, L1_gnn_b2, L1_gnn_emb, L1_gnn_adaptW, L1_gnn_gamma, L1_gnn_beta):
    import jax
    import jax.numpy as jnp

    def _L0_gnn_ref(x, edge_index, edge_weight):
        import jax, jax.numpy as jnp
        import numpy as np
        NUM_NODES = 12500
        src, dst = (edge_index[0], edge_index[1])
        msgs = x[src] * edge_weight[:, None]
        out = jax.ops.segment_sum(msgs, dst, num_segments=NUM_NODES)
        return out

    def _L1_gnn_ref(h, edge_index, edge_attr, distances, atom_z, node_mult, batch, W1, b1, W2, b2, emb, adaptW, gamma, beta):
        import jax, jax.numpy as jnp
        import numpy as np
        CUTOFF = 6.0
        LN_EPS = 1e-05
        src, dst = (edge_index[0], edge_index[1])
        N = h.shape[0]
        gate = jax.nn.silu(edge_attr @ W1.T + b1) @ W2.T + b2
        ei = emb[atom_z[src]]
        ej = emb[atom_z[dst]]
        adapt_logit = jnp.sum(ei * (ej @ adaptW.T), axis=-1, keepdims=True)
        gate = gate + adapt_logit
        cw = jnp.where(distances < CUTOFF, 0.5 * (jnp.cos(jnp.pi * distances / CUTOFF) + 1.0), 0.0)
        mj = node_mult[dst]
        msg = gate * h[dst] * (cw * mj)[:, None]
        agg = jax.ops.segment_sum(msg, src, num_segments=N)
        tot = jax.ops.segment_sum(mj, src, num_segments=N)
        agg = agg / jnp.clip(tot, 1e-08, None)[:, None]
        x = h + agg
        mu = jnp.mean(x, axis=-1, keepdims=True)
        var = jnp.mean(jnp.square(x - mu), axis=-1, keepdims=True)
        return (x - mu) / jnp.sqrt(var + LN_EPS) * gamma + beta

    def _L2_gnn_ref(soft_label, e, src, dst):
        import jax, jax.numpy as jnp
        import numpy as np
        N_NODES = 12500
        N_EDGES = 200000
        N_CLASSES = 48
        N = soft_label.shape[0]
        logits = e[:, 0]
        seg_max = jax.ops.segment_max(logits, dst, num_segments=N)
        seg_max = jnp.where(jnp.isfinite(seg_max), seg_max, 0.0)
        ex = jnp.exp(logits - seg_max[dst])
        seg_sum = jax.ops.segment_sum(ex, dst, num_segments=N)
        a = ex / seg_sum[dst]
        msg = soft_label[src] * a[:, None]
        rst = jax.ops.segment_sum(msg, dst, num_segments=N)
        return jax.nn.elu(rst)

    def _L3_gnn_ref(features, edge_weight, edge_index):
        import jax, jax.numpy as jnp
        import numpy as np
        NUM_LAYERS = 2
        N_NODES = 12500
        N_EDGES = 200000
        D_FEAT = 48

        def spmm(edge_index, edge_weight, x, n):
            src, dst = (edge_index[0], edge_index[1])
            msgs = x[src] * edge_weight[:, None]
            return jax.ops.segment_sum(msgs, dst, num_segments=n)
        n = features.shape[0]
        scale = 1.0 / (NUM_LAYERS + 1)
        avg = features * scale
        x = features
        for _ in range(NUM_LAYERS):
            x = spmm(edge_index, edge_weight, x, n)
            avg = avg + x * scale
        return avg
    edge_index = jnp.stack([src, dst])
    batch0 = jnp.zeros((12500,), jnp.int32)
    h = jnp.maximum(_layernorm(x, axis=-1), 0.0)
    x = x + _L0_gnn_ref(h, edge_index, edge_weight)
    h = jnp.maximum(_layernorm(x, axis=-1), 0.0)
    x = x + _L1_gnn_ref(h, edge_index, edge_attr_40, edge_weight, node_type_119, node_vec, batch0, L1_gnn_W1, L1_gnn_b1, L1_gnn_W2, L1_gnn_b2, L1_gnn_emb, L1_gnn_adaptW, L1_gnn_gamma, L1_gnn_beta)
    h = jnp.maximum(_layernorm(x, axis=-1), 0.0)
    x = x + _L2_gnn_ref(h, edge_weight1, src, dst)
    h = jnp.maximum(_layernorm(x, axis=-1), 0.0)
    x = x + _L3_gnn_ref(h, edge_weight, edge_index)
    return x

_drawn_inputs = setup_inputs


def setup_inputs(seed=0):
    import zlib

    import numpy as np

    out = dict(_drawn_inputs(seed))
    spreads = {'L1_gnn_gamma': (1.0, 0.2), 'L1_gnn_beta': (0.0, 0.1)}
    factors = {'edge_attr_40': 8.0,
     'edge_weight1': 3.609,
     'node_vec': 8.0,
     'L1_gnn_b1': 58.266,
     'L1_gnn_b2': 38.117,
     'L1_gnn_emb': 64.0,
     'L1_gnn_adaptW': 64.0}
    for name, (base, spread) in spreads.items():
        noise = np.random.default_rng([zlib.crc32(name.encode()), seed]).standard_normal(out[name].shape)
        drawn = base * np.exp(spread * noise) if base else spread * noise
        out[name] = jnp.asarray(drawn.astype(out[name].dtype))
    for name, factor in factors.items():
        out[name] = (out[name] * factor).astype(out[name].dtype)
    return out
```

```python
import concourse.bass as bass
from concourse import mybir
from contextlib import ExitStack

N = 12500
C = 48
E = 212500
R = 40
NEL = 119
GE = 32
P = 128
NB_BITS = 7
NB = -(-N // P)
NPAD = NB * P
NBW = NB + 2
G = 4
GB = 4
U = G * GB
NG = -(-E // (P * U)) * GB
T = NG * G
TURNS = NG // GB
GW = G * P
AHEAD = 2
TI = T + AHEAD * G
WB = 2
C0 = C + GE
CS = C + 1
CT = C + 2
K = 8
TRASH = NPAD
NR = NPAD + P
CUTOFF = 6.0
LN_EPS = 1e-5
BIG = 1e30
LAYERS = 2
ZB = 7
PI = 3.141592653589793


def gnn_kernel(nc, x, dst_cols, src_cols, dst_rows, src_rows, w_cols, logit_cols, logit_rows,
               attr_t, type_row, mult, w1_t, b1, w2e, emb, emb_t, adapt_t, gamma, beta, out):
    f32 = mybir.dt.float32
    i32 = mybir.dt.int32
    u16 = mybir.dt.uint16
    bf16 = mybir.dt.bfloat16
    ALU = mybir.AluOpType
    ACT = mybir.ActivationFunctionType
    X_AXIS = mybir.AxisListType.X
    ds = bass.ds

    with ExitStack() as ctx:
        def sb(name, shape, dt=f32):
            return ctx.enter_context(nc.sbuf_tensor(name, shape, dt))

        def sem(name):
            return ctx.enter_context(nc.semaphore(name))

        def dram(name, shape, dt=f32):
            return nc.dram_tensor(name, shape, dt, kind="Internal").ap()

        table0 = dram("table0", (NPAD, C0))
        table2 = dram("table2", (NPAD, CS))
        table3 = [dram(f"table3_{k}", (NPAD, C)) for k in range(LAYERS)]
        sums = [dram(f"sums{k}", (NR, CS)) for k in range(K)]
        src_row_dram = dram("src_row_dram", (NG, GW))
        ranges_dram = dram("ranges_dram", (TURNS, GB * 2), i32)

        nodes = sb("nodes", [P, NB, C])
        h = sb("h", [P, NB, C])
        acc = sb("acc", [P, NBW, CS])
        table = sb("table", [P, NBW, CT])
        scratch = sb("scratch", [P, NB * CS + 16])
        embq = sb("embq", [P, NBW, GE])
        iota = sb("iota", [P, NBW * P], u16)
        dstf = sb("dstf", [P, T])
        w = sb("w", [P, T])
        cw = sb("cw", [P, T])
        lg = sb("lg", [P, T])
        adapt = sb("adapt", [P, T])
        srow = sb("srow", [P, TI])
        ranges = sb("ranges", [1, NG * 2], i32)
        negnode = sb("negnode", [P, NBW])
        segmax = sb("segmax", [P, NBW])
        multc = sb("multc", [P, NB])
        gammab = sb("gammab", [P, C])
        betab = sb("betab", [P, C])
        w1s = sb("w1s", [R, C])
        b1s = sb("b1s", [C, 1])
        w2s = sb("w2s", [C + 1, C])
        lower = sb("lower", [P, P])
        trash = sb("trash", [P, 1])
        zeros = sb("zeros", [1, G * CT], bf16)
        idx = sb("idx", [P, U], i32)
        rows = sb("rows", [P, U, C0])
        onehot = sb("onehot", [P, G, WB * P])
        drow = sb("drow", [P, 2, GW], i32)
        lrow = sb("lrow", [P, 2, GW])
        attr = sb("attr", [R, 2, GW])
        hid = sb("hid", [C + 1, 2, GW])
        gate = sb("gate", [P, G, CS])
        msg = sb("msg", [P, G, CS])
        dup = sb("dup", [P, G])
        dmp = sb("dmp", [P, G])
        wmax = sb("wmax", [P, WB])
        dots = sb("dots", [P, G, GE])
        dist = scratch[:, 0:WB * GW].rearrange("p (b e) -> p b e", b=WB)
        onet = scratch[:, WB * GW:2 * WB * GW].rearrange("p (b e) -> p b e", b=WB)
        pen = scratch[:, 2 * WB * GW:3 * WB * GW].rearrange("p (b e) -> p b e", b=WB)
        same = scratch[:, 2 * WB * GW:2 * WB * GW + 2 * GW].rearrange("p (r g e) -> p r g e", r=2, g=G)
        junk = scratch[:, 3 * WB * GW:4 * WB * GW].rearrange("p (b e) -> p b e", b=WB)
        def ps(name, shape):
            return ctx.enter_context(nc.psum_tensor(name, shape, f32))

        psum_acc = ps("psum_acc", [P, WB, 512])
        psum_exp = [ps(f"psum_exp{r}", [P, 512]) for r in range(2)]
        psum_gate = ps("psum_gate", [P, 512])
        psum_comb = [ps(f"psum_comb{r}", [P, 512]) for r in range(2)]
        psum_hid = ps("psum_hid", [P, 512])

        zc = scratch[0:NEL, 0:2 * ZB * P].bitcast(i32).rearrange("p (r n) -> p r n", r=2)
        zhot = scratch[0:NEL, 2 * ZB * P:4 * ZB * P].rearrange("p (r n) -> p r n", r=2)
        typec = sb("typec", [P, 1])
        ea = sb("ea", [NEL, 2 * GE])
        embts = sb("embts", [GE, NEL])
        adapts = sb("adapts", [GE, GE])
        stat = sb("stat", [P, 4, NB])
        tbl_flat = table[:, :, :].rearrange("p b c -> p (b c)")
        acc_flat = acc[:, :, :].rearrange("p b c -> p (b c)")
        h_flat = h[:, :, :].rearrange("p b c -> p (b c)")
        int_a = tbl_flat[:, 0:2 * T // 2].bitcast(i32)
        int_b = tbl_flat[:, T:2 * T].bitcast(i32)
        int_c = tbl_flat[:, 2 * T:3 * T].bitcast(i32)
        emb_rows = rows
        embst = acc_flat[:, 0:NB * GE].rearrange("p (b c) -> p b c", c=GE)
        dr_i = h_flat[0:TURNS, 0:GB * GW].bitcast(i32)
        sr_i = h_flat[0:TURNS, GB * GW:2 * GB * GW].bitcast(i32)
        wk_i = stat[:, :, :].rearrange("p a b -> p (a b)").bitcast(i32)

        def by_partition(t, c):
            return t.rearrange("(p b) c -> p b c", p=P)[:, :, c[0]:c[1]]

        def layernorm_relu(link, nv, na, s_var, s_std, turn, src, dst, mul=None, add=None):
            d3 = scratch[:, 0:NB * C].rearrange("p (b c) -> p b c", c=C)
            s, v, r = stat[:, 0, :], stat[:, 1, :], stat[:, 2, :]
            bc = lambda a: a.unsqueeze(2).to_broadcast([P, NB, C])
            link(nv.tensor_reduce(out=s, in_=src, axis=X_AXIS, op=ALU.add))
            link(nv.tensor_scalar(s, s, 1.0 / C, None, ALU.mult))
            link(nv.tensor_tensor(dst, src, bc(s), ALU.subtract))
            link(nv.tensor_tensor(d3, dst, dst, ALU.mult))
            link(nv.tensor_reduce(out=v, in_=d3, axis=X_AXIS, op=ALU.add))
            nv.tensor_scalar(v, v, 1.0 / C, LN_EPS, ALU.mult, ALU.add).then_inc(s_var, 1)
            nv.wait_ge(s_std, turn + 1)
            link(nv.reciprocal(r, stat[:, 3, :]))
            if mul is None:
                link(nv.scalar_tensor_tensor(out=dst, in0=dst, scalar=0.0, in1=bc(r), op0=ALU.max, op1=ALU.mult))
            else:
                link(nv.tensor_tensor(dst, dst, bc(r), ALU.mult))
                link(nv.tensor_tensor(dst, dst, mul.unsqueeze(1).to_broadcast([P, NB, C]), ALU.mult))
                link(nv.tensor_tensor(dst, dst, add.unsqueeze(1).to_broadcast([P, NB, C]), ALU.add))

        def std(act, s_var, s_std, turn):
            act.wait_ge(s_var, turn + 1)
            nc.scalar.activation(stat[:, 3, :], stat[:, 1, :], ACT.Sqrt).then_inc(s_std, 1)

        def chain(eng, name):
            s, n = sem(name), [0]

            def link(instruction):
                n[0] += 1
                instruction.then_inc(s, 1)
                eng.wait_ge(s, n[0])
            return link

        nv = nc.vector

        s_x = sem("s_x"); s_ints = sem("s_ints"); s_rowints = sem("s_rowints"); s_w = sem("s_w")
        s_lg = sem("s_lg"); s_small = sem("s_small"); s_consts = sem("s_consts")
        s_srowd = sem("s_srowd"); s_srowout = sem("s_srowout"); s_ranged = sem("s_ranged")
        s_rangeout = sem("s_rangeout"); s_rangein = sem("s_rangein")
        s_zin = [sem(f"s_zin{r}") for r in range(2)]
        s_zhot = sem("s_zhot"); s_zmm = sem("s_zmm"); s_zout = sem("s_zout")
        s_ea = sem("s_ea"); s_eamm = sem("s_eamm")
        s_var = sem("s_var"); s_std = sem("s_std")
        s_h0 = sem("s_h0"); s_table0 = sem("s_table0"); s_sin = sem("s_sin"); s_sinin = sem("s_sinin")
        s_zero = sem("s_zero"); s_cleared = sem("s_cleared")
        ZT = NB // ZB
        with nc.Block() as block:
            @block.sync
            def _(sp):
                sp.dma_start(int_a, src_cols).then_inc(s_ints, 16)
                sp.dma_start(int_b, dst_cols).then_inc(s_ints, 16)
                sp.dma_start(dr_i, dst_rows.rearrange("(q j) e -> q (j e)", j=GB)).then_inc(s_rowints, 16)
                sp.dma_start(sr_i, src_rows.rearrange("(q j) e -> q (j e)", j=GB)).then_inc(s_rowints, 16)
                sp.dma_start(w[:, :], w_cols).then_inc(s_w, 16)
                sp.dma_start(nodes[:, :, :].rearrange("p b c -> p (b c)"), x).then_inc(s_x, 16)
                sp.dma_start(lg[:, :], logit_cols).then_inc(s_lg, 16)
                sp.wait_ge(s_srowd, 1)
                sp.dma_start(src_row_dram.rearrange("(q j) e -> q (j e)", j=GB),
                             scratch[0:TURNS, 2 * GB * GW - GB * GW:2 * GB * GW]).then_inc(s_srowout, 16)
                sp.wait_ge(s_ranged, 1)
                sp.dma_start(ranges_dram, idx[0:TURNS, 0:2 * GB]).then_inc(s_rangeout, 16)
                sp.wait_ge(s_rangeout, 16)
                sp.dma_start(ranges[0:1, :], ranges_dram.rearrange("q j -> (q j)").unsqueeze(0)).then_inc(s_rangein, 16)
                sp.wait_ge(s_rangein, 16)
                sp.wait_ge(s_srowout, 16)
                sp.wait_ge(s_lg, 16)

            @block.gpsimd
            def _(pool):
                nc.gpsimd.iota(iota[:, :], pattern=[[1, NBW * P]], base=0, channel_multiplier=0).then_inc(s_consts, 1)
                nc.gpsimd.memset(lower[:, :], 1.0).then_inc(s_consts, 1)
                pool.wait_ge(s_consts, 2)
                nc.gpsimd.affine_select(out=lower[:, :], in_=lower[:, :], compare_op=ALU.is_gt, fill=0.0,
                                        base=0, pattern=[[-1, P]], channel_multiplier=1).then_inc(s_consts, 1)

            @block.scalar
            def _(act):
                act.dma_start(multc[:, :], mult).then_inc(s_small, 16)
                act.dma_start(gammab[:, :], gamma.partition_broadcast(P)).then_inc(s_small, 16)
                act.dma_start(betab[:, :], beta.partition_broadcast(P)).then_inc(s_small, 16)
                act.dma_start(w1s[:, :], w1_t).then_inc(s_small, 16)
                act.dma_start(b1s[:, :], b1).then_inc(s_small, 16)
                act.dma_start(w2s[:, :], w2e).then_inc(s_small, 16)
                act.dma_start(ea[:, 0:GE], emb).then_inc(s_small, 16)
                act.dma_start(embts[:, :], emb_t).then_inc(s_small, 16)
                act.dma_start(adapts[:, :], adapt_t).then_inc(s_small, 16)
                act.wait_ge(s_small, 9 * 16)

            @block.vector
            def _(dve):
                link = chain(dve, "s_setup_chain")
                nv.memset(zeros[:, :], 0.0)
                nv.memset(acc_flat, 0.0)
                nv.memset(segmax[:, :], -BIG)
                nv.memset(embq[:, :, :], 0.0)
                nv.memset(srow[:, T:TI], 0.0)
                nv.memset(hid[:, :, :], 1.0)
                nv.memset(gate[:, :, :], 1.0)
                dve.wait_ge(s_ints, 32)
                nv.tensor_copy(dstf[:, :], int_b)
                link(nv.tensor_scalar(int_c, int_a, NB_BITS, None, ALU.logical_shift_right))
                link(nv.tensor_scalar(int_a, int_a, P - 1, None, ALU.bitwise_and))
                link(nv.scalar_tensor_tensor(out=srow[:, 0:T], in0=int_a, scalar=float(NB), in1=int_c, op0=ALU.mult, op1=ALU.add))
                dve.wait_ge(s_rowints, 32)
                tmp = scratch[0:TURNS, 0:GB * GW].bitcast(i32)
                link(nv.tensor_scalar(tmp, sr_i, NB_BITS, None, ALU.logical_shift_right))
                link(nv.tensor_scalar(sr_i, sr_i, P - 1, None, ALU.bitwise_and))
                nv.scalar_tensor_tensor(out=scratch[0:TURNS, GB * GW:2 * GB * GW], in0=sr_i, scalar=float(NB),
                                        in1=tmp, op0=ALU.mult, op1=ALU.add).then_inc(s_srowd, 1)
                d4 = dr_i.rearrange("q (j e) -> q j e", j=GB)
                lo = wk_i[0:TURNS, 0:GB]
                hi = wk_i[0:TURNS, GB:2 * GB]
                link(nv.tensor_reduce(out=lo, in_=d4, axis=X_AXIS, op=ALU.min))
                link(nv.tensor_reduce(out=hi, in_=d4, axis=X_AXIS, op=ALU.max))
                link(nv.tensor_scalar(lo, lo, NB_BITS, None, ALU.logical_shift_right))
                link(nv.tensor_scalar(hi, hi, NB_BITS, None, ALU.logical_shift_right))
                pairs = idx[0:TURNS, 0:2 * GB].rearrange("q (j k) -> q j k", k=2)
                link(nv.tensor_copy(pairs[:, :, 0], lo))
                link(nv.tensor_scalar(pairs[:, :, 1], hi, 1.0, None, ALU.add))
                link(nv.memset(stat[:, 3, 0:1], 0.0))
                dve.wait_ge(s_rangein, 0)
                nv.memset(stat[:, 3, 1:2], 0.0).then_inc(s_ranged, 1)

        with nc.Block() as block:
            @block.sync
            def _(sp):
                for c in range(K):
                    sp.dma_start(sums[c].rearrange("(p r) c -> p (r c)", p=P), acc_flat[:, 0:NR // P * CS]).then_inc(s_cleared, 16)
                sp.wait_ge(s_cleared, 16 * K)

            @block.gpsimd
            def _(pool):
                nc.gpsimd.iota(int_a[:, 0:1], pattern=[[0, 1]], base=0, channel_multiplier=1).then_inc(s_consts, 1)
                nc.gpsimd.iota(int_a[:, 1:1 + NBW], pattern=[[-P, NBW]], base=0, channel_multiplier=-1).then_inc(s_consts, 1)
                nc.gpsimd.iota(int_a[:, 1 + NBW:2 + NBW], pattern=[[0, 1]], base=TRASH, channel_multiplier=1).then_inc(s_consts, 1)

            @block.vector
            def _(dve):
                link = chain(dve, "s_const_chain")
                dve.wait_ge(s_consts, 6)
                link(nv.tensor_copy(typec[:, :], int_a[:, 0:1]))
                link(nv.tensor_copy(negnode[:, :], int_a[:, 1:1 + NBW]))
                link(nv.tensor_copy(trash[:, :], int_a[:, 1 + NBW:2 + NBW]))
                a, b = int_c.bitcast(f32), int_b
                k12 = 2 * CUTOFF
                link(nv.tensor_scalar(a, w[:, :], -1.0, None, ALU.mult))
                link(nv.tensor_tensor(a, a, w[:, :], ALU.max))
                link(nv.tensor_scalar(b, a, 1.0 / k12, None, ALU.mult))
                link(nv.scalar_tensor_tensor(out=a, in0=b, scalar=-k12, in1=a, op0=ALU.mult, op1=ALU.add))
                c = cw[:, :]
                link(nv.tensor_scalar(c, a, -1.0, None, ALU.mult))
                link(nv.tensor_tensor(a, a, c, ALU.max))
                link(nv.tensor_scalar(c, a, -1.0, k12, ALU.mult, ALU.add))
                link(nv.tensor_tensor(a, a, c, ALU.min))
                nv.tensor_scalar(a, a, -PI / CUTOFF, PI / 2, ALU.mult, ALU.add).then_inc(s_sinin, 1)
                dve.wait_ge(s_sin, 1)
                link(nv.tensor_scalar(c, c, 0.5, 0.5, ALU.mult, ALU.add))
                link(nv.scalar_tensor_tensor(out=c, in0=w[:, :], scalar=CUTOFF, in1=c, op0=ALU.is_lt, op1=ALU.mult))
                dve.wait_ge(s_eamm, 1)
                nv.tensor_copy(ea[:, GE:2 * GE], psum_gate[0:NEL, 0:GE]).then_inc(s_ea, 1)
                for q in range(ZT):
                    dve.wait_ge(s_zin[q % 2], 16 * (q // 2 + 1))
                    if q >= 2:
                        dve.wait_ge(s_zmm, q - 1)
                    nv.tensor_scalar(zhot[:, q % 2, :], zc[:, q % 2, :], typec[0:NEL, 0:1], None,
                                     ALU.is_equal).then_inc(s_zhot, 1)
                dve.wait_ge(s_zout, ZT)
                layernorm_relu(link, nv, None, s_var, s_std, 0, nodes[:, :, :], h[:, :, :])
                nv.memset(stat[:, 0, 0:1], 0.0).then_inc(s_h0, 1)

            @block.tensor
            def _(pe):
                nc.tensor.matmul(psum_gate[0:NEL, 0:GE], embts[:, :], adapts[:, :], start=True, stop=True).then_inc(s_eamm, 1)
                pe.wait_ge(s_ea, 1)
                for q in range(ZT):
                    pe.wait_ge(s_zhot, q + 1)
                    if q >= 2:
                        pe.wait_ge(s_zout, q - 1)
                    for b in range(ZB):
                        last = nc.tensor.matmul(psum_exp[q % 2][:, b * 2 * GE:(b + 1) * 2 * GE],
                                                zhot[:, q % 2, b * P:(b + 1) * P], ea[:, :], start=True, stop=True)
                    last.then_inc(s_zmm, 1)

            @block.scalar
            def _(act):
                s_half = sem("s_half")
                act.wait_ge(s_sinin, 1)
                nc.scalar.activation(cw[:, :], int_c.bitcast(f32), ACT.Sin).then_inc(s_sin, 1)
                for q in range(min(2, ZT)):
                    act.dma_start(zc[:, q, :], type_row[0, q * ZB * P:(q + 1) * ZB * P].partition_broadcast(NEL)).then_inc(s_zin[q], 16)
                act.wait_ge(s_cleared, 16 * K)
                for q in range(ZT):
                    act.wait_ge(s_zmm, q + 1)
                    pv = psum_exp[q % 2][:, 0:ZB * 2 * GE].rearrange("p (b c) -> p b c", c=2 * GE)
                    nc.scalar.copy(embst[:, q * ZB:(q + 1) * ZB, :], pv[:, :, 0:GE]).then_inc(s_half, 1)
                    nc.scalar.copy(embq[:, q * ZB:(q + 1) * ZB, :], pv[:, :, GE:2 * GE]).then_inc(s_zout, 1)
                    if q + 2 < ZT:
                        act.dma_start(zc[:, q % 2, :], type_row[0, (q + 2) * ZB * P:(q + 3) * ZB * P].partition_broadcast(NEL)).then_inc(s_zin[q % 2], 16)
                act.wait_ge(s_half, ZT)
                act.dma_start(by_partition(table0, (C, C0)), embst).then_inc(s_table0, 16)
                std(act, s_var, s_std, 0)
                act.wait_ge(s_h0, 1)
                act.dma_start(by_partition(table0, (0, C)), h[:, :, :]).then_inc(s_table0, 16)
                act.wait_ge(s_table0, 32)

        s_rows = [sem(f"s_rows{u}") for u in range(U)]
        s_hot = [sem(f"s_hot{u}") for u in range(G)]
        s_prod = sem("s_prod")
        s_added = sem("s_added")
        s_dist = sem("s_dist")
        s_onet = sem("s_onet")
        s_pen = sem("s_pen")
        s_exp = sem("s_exp")
        s_wmax = sem("s_wmax")
        s_maxed = sem("s_maxed")
        s_dots = sem("s_dots")
        s_closed = sem("s_closed")
        wn_dve = nc.vector.alloc_register("dve_windows")
        wn_pe = nc.tensor.alloc_register("pe_windows")

        def spmm_pass(order, name, src_table, cols, weights, first):
            s_idx = sem(name + "_idx")
            s_idx_seen = sem(name + "_idx_seen")
            s_done = sem(name + "_done")
            s_bcast = [sem(f"{name}_bcast{r}") for r in range(2)] if first else None
            before = order * TURNS * 16
            s_staged = sem(name + "_staged")
            width = src_table.shape[1]
            s_clear = sem(name + "_clear")
            with nc.Block() as block:
                @block.gpsimd
                def _(pool):
                    with pool.Fori(0, TURNS) as i:
                        for j in range(GB):
                            pool.wait_ge(s_idx, i * GB + (j + 1))
                            pool.sem_inc(s_idx_seen, 1)
                            for u in range(j * G, (j + 1) * G):
                                pool.indirect_dma_start(
                                    out=rows[:, u, 0:width], out_offset=None, in_=src_table,
                                    in_offset=bass.IndirectOffsetOnAxis(ap=idx[:, u:u + 1], axis=0)).then_inc(s_rows[u], 16)

                if first:
                    @block.sync
                    def _(sp):
                        with sp.Fori(0, TURNS) as i:
                            for j in range(GB):
                                sp.wait_ge(s_done, i * GB + (j + GB - 1))
                                sp.dma_start(drow[:, j % 2, :], dst_rows[ds(i * GB + j, 1), :].squeeze(0).partition_broadcast(P)).then_inc(s_bcast[j % 2], 16)
                                sp.dma_start(lrow[:, j % 2, :], logit_rows[ds(i * GB + j, 1), :].squeeze(0).partition_broadcast(P)).then_inc(s_bcast[j % 2], 16)

                @block.scalar
                def _(act):
                    def stage(slot, column):
                        nc.scalar.copy(idx[:, slot * G:(slot + 1) * G], srow[:, ds(column, G)]).then_inc(s_idx, 1)

                    for j in range(AHEAD):
                        stage(j, j * G)
                    wn = act.alloc_register(name + "_act_windows")
                    act.reg_mov(wn, 0)
                    with act.Fori(0, TURNS) as i:
                        for j in range(GB):
                            act.wait_ge(s_done, i * GB + (j + AHEAD + 1))
                            act.sem_inc(s_staged, 1)
                            stage((j + AHEAD) % GB, i * U + (j + AHEAD) * G)
                            if not first:
                                continue
                            lo = act.value_load(ranges[0:1, ds((i * GB + j) * 2, 1)], min_val=0, max_val=NB - 1)
                            n = act.value_load(ranges[0:1, ds((i * GB + j) * 2 + 1, 1)], min_val=1, max_val=NB)
                            act.wait_ge(s_bcast[j % 2], i * (2 * 16 * GB // 2) + 32 * (j // 2 + 1))
                            act.sem_inc(s_staged, 1)
                            with act.Fori(lo, n, WB) as k:
                                act.wait_ge(s_pen, act.snap(wn))
                                act.sem_inc(s_staged, 1)
                                for b in range(WB):
                                    nc.scalar.activation(dist[:, b, :], drow[:, j % 2, :], ACT.Abs,
                                                         bias=negnode[:, ds(k + b, 1)]).then_inc(s_dist, 1)
                                act.wait_ge(s_dist, act.snap(wn) * WB + WB)
                                act.sem_inc(s_staged, 1)
                                act.wait_ge(s_exp, act.snap(wn))
                                nc.scalar.activation(onet, dist, ACT.Relu, scale=-1.0, bias=1.0).then_inc(s_onet, 1)
                                act.wait_ge(s_wmax, act.snap(wn) * WB)
                                nc.scalar.activation(pen, dist, ACT.Copy, scale=-BIG).then_inc(s_pen, 1)
                                act.reg_add(wn, wn, 1)

                @block.vector
                def _(dve):
                    nv.memset(acc_flat, 0.0).then_inc(s_clear, 1)
                    dve.wait_ge(s_clear, 1)
                    dve.sem_inc(s_done, GB)
                    wn = wn_dve
                    if first:
                        dve.reg_mov(wn, 0)
                    with dve.Fori(0, TURNS) as i:
                        for j in range(GB):
                            lo = dve.value_load(ranges[0:1, ds((i * GB + j) * 2, 1)], min_val=0, max_val=NB - 1)
                            n = dve.value_load(ranges[0:1, ds((i * GB + j) * 2 + 1, 1)], min_val=1, max_val=NB)
                            with dve.Fori(lo, n, WB) as k:
                                blk = k
                                for u in range(G):
                                    t = i * U + (j * G + u)
                                    nv.tensor_scalar(onehot[:, u, :], iota[:, ds(blk * P, WB * P)], dstf[:, ds(t, 1)],
                                                     weights[:, ds(t, 1)], ALU.is_equal, ALU.mult).then_inc(s_hot[u], 1)
                                if first:
                                    dve.wait_ge(s_pen, dve.snap(wn) + 1)
                                    dve.sem_inc(s_staged, 1)
                                    for b in range(WB):
                                        nv.tensor_tensor_reduce(out=junk[:, b, :], in0=pen[:, b, :], in1=lrow[:, j % 2, :], scale=1.0,
                                                                scalar=-BIG, op0=ALU.add, op1=ALU.max,
                                                                accum_out=wmax[:, b:b + 1]).then_inc(s_wmax, 1)
                                    dve.wait_ge(s_maxed, dve.snap(wn))
                                    dve.wait_ge(s_wmax, dve.snap(wn) * WB + WB)
                                    nv.tensor_tensor(segmax[:, ds(blk, WB)], segmax[:, ds(blk, WB)], wmax[:, :],
                                                     ALU.max).then_inc(s_maxed, 1)
                                dve.wait_ge(s_added, dve.snap(wn))
                                dve.wait_ge(s_prod, dve.snap(wn) + 1)
                                last = nv.tensor_tensor(acc[:, ds(blk, WB), 0:cols], acc[:, ds(blk, WB), 0:cols],
                                                        psum_acc[:, :, 0:cols], ALU.add)
                                last.then_inc(s_added, 1)
                                dve.reg_add(wn, wn, 1)
                            if first:
                                dve.wait_ge(s_closed, i * GB + (j + 1))
                                pq = psum_exp[j % 2][:, 0:G * GE].rearrange("p (g c) -> p g c", c=GE)
                                nv.tensor_tensor(dots[:, :, :], rows[:, j * G:(j + 1) * G, C:C0], pq, ALU.mult).then_inc(s_dots, 1)
                                dve.wait_ge(s_dots, i * GB + (j + 1))
                                nv.tensor_reduce(out=adapt[:, ds(i * U + j * G, G)], in_=dots[:, :, :], axis=X_AXIS,
                                                 op=ALU.add).then_inc(s_done, 1)
                            else:
                                dve.sem_inc(s_done, 1)

                @block.tensor
                def _(pe):
                    wn = wn_pe
                    if first:
                        pe.reg_mov(wn, 0)
                    with pe.Fori(0, TURNS) as i:
                        for j in range(GB):
                            lo = pe.value_load(ranges[0:1, ds((i * GB + j) * 2, 1)], min_val=0, max_val=NB - 1)
                            n = pe.value_load(ranges[0:1, ds((i * GB + j) * 2 + 1, 1)], min_val=1, max_val=NB)
                            if first:
                                pe.wait_ge(s_done, i * GB + (j + GB - 1))
                                nc.tensor.matmul(psum_exp[j % 2][:, 0:G * GE], zeros[0:1, 0:P], zeros[0:1, 0:G * GE],
                                                 start=True, stop=False)
                            with pe.Fori(lo, n, WB) as k:
                                if first:
                                    pe.wait_ge(s_onet, pe.snap(wn) + 1)
                                    for u in range(G):
                                        for b in range(WB):
                                            last = nc.tensor.matmul(psum_exp[j % 2][:, u * GE:(u + 1) * GE],
                                                                    onet[:, b, u * P:(u + 1) * P],
                                                                    embq[:, ds(k + b, 1), :].rearrange("p b c -> p (b c)"),
                                                                    start=False, stop=False)
                                    last.then_inc(s_exp, 1)
                                for u in range(G):
                                    pe.wait_ge(s_rows[j * G + u], i * 16 + (before + 16))
                                    pe.wait_ge(s_hot[u], pe.snap(wn) + 1)
                                    for b in range(WB):
                                        last = nc.tensor.matmul(psum_acc[:, b, 0:cols], onehot[:, u, b * P:(b + 1) * P],
                                                                rows[:, j * G + u, 0:cols], start=(u == 0), stop=(u == G - 1))
                                last.then_inc(s_prod, 1)
                                pe.reg_add(wn, wn, 1)
                            if first:
                                nc.tensor.matmul(psum_exp[j % 2][:, 0:G * GE], zeros[0:1, 0:P], zeros[0:1, 0:G * GE],
                                                 start=False, stop=True).then_inc(s_closed, 1)

        spmm_pass(0, "l0", table0, C, w, True)

        s_var1 = sem("s_var1"); s_std1 = sem("s_std1")
        with nc.Block() as block:
            @block.vector
            def _(dve):
                link = chain(dve, "s_epi0_chain")
                link(nv.memset(table[:, NB:NBW, :], 0.0))
                link(nv.tensor_tensor(nodes[:, :, :], nodes[:, :, :], acc[:, 0:NB, 0:C], ALU.add))
                layernorm_relu(link, nv, None, s_var1, s_std1, 0, nodes[:, :, :], h[:, :, :])
                link(nv.tensor_tensor(table[:, 0:NB, 0:C], h[:, :, :], multc[:, :].unsqueeze(2).to_broadcast([P, NB, C]), ALU.mult))
                link(nv.tensor_copy(table[:, 0:NB, C], multc[:, :]))
                link(nv.tensor_copy(table[:, 0:NB, C + 1], segmax[:, 0:NB]))

            @block.scalar
            def _(act):
                std(act, s_var1, s_std1, 0)

        s_in = [sem(f"l1_in{r}") for r in range(2)]
        s_same = sem("l1_same"); s_dup = sem("l1_dup"); s_dmp = sem("l1_dmp"); s_idx1 = sem("l1_idx")
        s_hid = sem("l1_hid"); s_silu = sem("l1_silu"); s_dist1 = sem("l1_dist"); s_onet1 = sem("l1_onet")
        s_exp1 = sem("l1_exp"); s_mlp = sem("l1_mlp"); s_gate = sem("l1_gate")
        s_msg = sem("l1_msg")
        s_comb = sem("l1_comb")
        s_out = sem("l1_out")
        s_free = sem("l1_free")
        s_scat = [sem(f"l1_scat{c}") for c in range(K)]
        s_landed = sem("l1_landed")
        s_turn = sem("l1_turn"); s_seen = sem("l1_seen")
        pairk = K // G
        with nc.Block() as block:
            @block.sync
            def _(sp):
                with sp.Fori(0, TURNS) as i:
                    for j in range(GB):
                        sp.wait_ge(s_msg, i * GB + (j + 1))
                        g = i * GB + j
                        sp.dma_start(drow[:, j % 2, :], dst_rows[ds(g, 1), :].squeeze(0).partition_broadcast(P)).then_inc(s_in[j % 2], 16)
                        sp.dma_start(lrow[:, j % 2, :], src_row_dram[ds(g, 1), :].squeeze(0).partition_broadcast(P)).then_inc(s_in[j % 2], 16)
                        sp.dma_start(attr[:, j % 2, :], attr_t[:, ds(g * GW, GW)]).then_inc(s_in[j % 2], 16)

            def inputs_here(eng, i, j):
                eng.wait_ge(s_in[j % 2], i * (48 * GB // 2) + 48 * (j // 2 + 1))

            @block.vector
            def _(dve):
                dve.sem_inc(s_msg, 2)
                with dve.Fori(0, TURNS) as i:
                    for j in range(GB):
                        g = i * GB + j
                        inputs_here(dve, i, j)
                        for u in range(G):
                            nv.tensor_scalar(same[:, j % 2, u, :], lrow[:, j % 2, u * P:(u + 1) * P],
                                             srow[:, ds(i * U + (j * G + u), 1)], None, ALU.is_equal).then_inc(s_same, 1)
                        dve.wait_ge(s_same, g * G + G)
                        dve.sem_inc(s_seen, 1)
                        for u in range(G):
                            nv.tensor_tensor_reduce(out=onehot[:, u, 0:P], in0=same[:, j % 2, u, :], in1=lower[:, :], scale=1.0, scalar=0.0,
                                                    op0=ALU.mult, op1=ALU.max, accum_out=dup[:, u:u + 1]).then_inc(s_dup, 1)
                        dve.wait_ge(s_dup, g * G + G)
                        nv.scalar_tensor_tensor(out=dmp[:, :], in0=srow[:, ds(i * U + j * G, G)], scalar=trash[:, 0:1],
                                                in1=dup[:, :], op0=ALU.subtract, op1=ALU.mult).then_inc(s_dmp, 1)
                        dve.wait_ge(s_dmp, g + 1)
                        dve.wait_ge(s_landed, g + (GB - 1))
                        nv.tensor_tensor(idx[:, j * G:(j + 1) * G], srow[:, ds(i * U + j * G, G)], dmp[:, :], ALU.subtract).then_inc(s_idx1, 1)
                        dve.wait_ge(s_mlp, g + 1)
                        for u in range(G):
                            t = i * U + (j * G + u)
                            nv.tensor_scalar(gate[:, u, 0:C], psum_gate[:, u * C:(u + 1) * C], adapt[:, ds(t, 1)],
                                             cw[:, ds(t, 1)], ALU.add, ALU.mult).then_inc(s_gate, 1)
                        ph = psum_exp[j % 2][:, 0:G * CT].rearrange("p (g c) -> p g c", c=CT)
                        nv.tensor_tensor(lg[:, ds(i * U + j * G, G)], lg[:, ds(i * U + j * G, G)], ph[:, :, C + 1], ALU.subtract)
                        dve.wait_ge(s_gate, g * G + G)
                        nv.tensor_tensor(msg[:, :, :], gate[:, :, :], ph[:, :, 0:CS], ALU.mult).then_inc(s_msg, 1)

            @block.tensor
            def _(pe):
                wn = pe.alloc_register("l1_pe_windows")
                pe.reg_mov(wn, 0)

                def combine(i, j):
                    g = i * GB + j
                    pe.wait_ge(s_msg, g + 3)
                    pe.wait_ge(s_free, g + 1)
                    for u in range(G):
                        last = nc.tensor.matmul(psum_comb[j % 2][:, u * CS:(u + 1) * CS], same[:, j % 2, u, :], msg[:, u, :],
                                                start=True, stop=True)
                    last.then_inc(s_comb, 1)

                with pe.Fori(0, TURNS) as i:
                    for j in range(GB):
                        g = i * GB + j
                        lo = pe.value_load(ranges[0:1, ds(g * 2, 1)], min_val=0, max_val=NB - 1)
                        n = pe.value_load(ranges[0:1, ds(g * 2 + 1, 1)], min_val=1, max_val=NB)
                        inputs_here(pe, i, j)
                        pe.sem_inc(s_seen, 1)
                        nc.tensor.matmul(psum_hid[0:C, :], w1s[:, :], attr[:, j % 2, :], start=True, stop=True).then_inc(s_hid, 1)
                        pe.wait_ge(s_msg, g + 1)
                        nc.tensor.matmul(psum_exp[j % 2][:, 0:G * CT], zeros[0:1, 0:P], zeros[0:1, 0:G * CT], start=True, stop=False)
                        with pe.Fori(lo, n, WB) as k:
                            pe.wait_ge(s_onet1, pe.snap(wn) + 1)
                            for u in range(G):
                                for b in range(WB):
                                    last = nc.tensor.matmul(psum_exp[j % 2][:, u * CT:(u + 1) * CT], onet[:, b, u * P:(u + 1) * P],
                                                            table[:, ds(k + b, 1), :].rearrange("p b c -> p (b c)"),
                                                            start=False, stop=False)
                            last.then_inc(s_exp1, 1)
                            pe.reg_add(wn, wn, 1)
                        nc.tensor.matmul(psum_exp[j % 2][:, 0:G * CT], zeros[0:1, 0:P], zeros[0:1, 0:G * CT], start=False, stop=True)
                        if j:
                            combine(i, j - 1)
                        pe.wait_ge(s_silu, g + 1)
                        for u in range(G):
                            last = nc.tensor.matmul(psum_gate[:, u * C:(u + 1) * C], hid[:, j % 2, u * P:(u + 1) * P], w2s[:, :],
                                                    start=True, stop=True)
                        last.then_inc(s_mlp, 1)
                    combine(i, GB - 1)

            @block.scalar
            def _(act):
                act.sem_inc(s_free, 2)
                wn = act.alloc_register("l1_act_windows")
                act.reg_mov(wn, 0)

                def hand_over(i, j):
                    g = i * GB + j
                    act.wait_ge(s_comb, g + 1)
                    act.sem_inc(s_seen, 1)
                    act.wait_ge(s_landed, g + (GB - 1))
                    nc.scalar.activation(rows[:, j * G:(j + 1) * G, 0:CS], psum_comb[j % 2][:, 0:G * CS].rearrange("p (g c) -> p g c", c=CS),
                                         ACT.Copy).then_inc(s_free, 1)

                with act.Fori(0, TURNS) as i:
                    for j in range(GB):
                        g = i * GB + j
                        lo = act.value_load(ranges[0:1, ds(g * 2, 1)], min_val=0, max_val=NB - 1)
                        n = act.value_load(ranges[0:1, ds(g * 2 + 1, 1)], min_val=1, max_val=NB)
                        inputs_here(act, i, j)
                        act.sem_inc(s_seen, 1)
                        with act.Fori(lo, n, WB) as k:
                            act.wait_ge(s_onet1, act.snap(wn))
                            act.sem_inc(s_seen, 1)
                            for b in range(WB):
                                nc.scalar.activation(dist[:, b, :], drow[:, j % 2, :], ACT.Abs,
                                                     bias=negnode[:, ds(k + b, 1)]).then_inc(s_dist1, 1)
                            act.wait_ge(s_dist1, act.snap(wn) * WB + WB)
                            act.sem_inc(s_seen, 1)
                            act.wait_ge(s_exp1, act.snap(wn))
                            nc.scalar.activation(onet, dist, ACT.Relu, scale=-1.0, bias=1.0).then_inc(s_onet1, 1)
                            act.reg_add(wn, wn, 1)
                        act.wait_ge(s_hid, g + 1)
                        nc.scalar.activation(hid[0:C, j % 2, :], psum_hid[0:C, :], ACT.Silu, bias=b1s[:, 0:1]).then_inc(s_silu, 1)
                        if j:
                            hand_over(i, j - 1)
                    hand_over(i, GB - 1)

            @block.gpsimd
            def _(pool):
                pool.sem_inc(s_landed, GB)
                with pool.Fori(0, TURNS) as i:
                    for j in range(GB):
                        g = i * GB + j
                        pool.wait_ge(s_free, g + 3)
                        pool.sem_inc(s_turn, 1)
                        pool.wait_ge(s_idx1, g + 1)
                        pool.sem_inc(s_turn, 1)
                        for u in range(j * G, (j + 1) * G):
                            c = u % K
                            pool.wait_ge(s_scat[c], i * (16 * U // K) + 16 * (u // K))
                            pool.sem_inc(s_turn, 1)
                            pool.indirect_dma_start(out=sums[c], out_offset=bass.IndirectOffsetOnAxis(ap=idx[:, u:u + 1], axis=0),
                                                    in_=rows[:, u, 0:CS], in_offset=None, compute_op=ALU.add).then_inc(s_scat[c], 16)
                        pool.sem_inc(s_landed, 1)
                for c in range(K):
                    pool.wait_ge(s_scat[c], 16 * T // K)

        s_var2 = sem("s_var2"); s_std2 = sem("s_std2"); s_exped = sem("s_exped")
        s_part = [sem(f"s_part{r}") for r in range(3)]
        s_used = sem("s_used"); s_t2 = sem("s_t2"); s_t2out = sem("s_t2out")
        n49 = NB * CS
        parts = [tbl_flat[:, 0:n49], scratch[:, 0:n49]]
        flat_acc = acc_flat[:, 0:n49]
        t2 = tbl_flat[:, 0:n49].rearrange("p (b c) -> p b c", c=CS)
        with nc.Block() as block:
            @block.sync
            def _(sp):
                sp.dma_start(flat_acc, sums[0][0:NPAD, :].rearrange("(p b) c -> p (b c)", p=P)).then_inc(s_part[2], 16)
                for c in range(1, K):
                    if c >= 3:
                        sp.wait_ge(s_used, c - 2)
                    sp.dma_start(parts[c % 2], sums[c][0:NPAD, :].rearrange("(p b) c -> p (b c)", p=P)).then_inc(s_part[c % 2], 16)
                sp.wait_ge(s_t2, 1)
                sp.dma_start(table2.rearrange("(p b) c -> p (b c)", p=P), tbl_flat[:, 0:n49]).then_inc(s_t2out, 16)
                sp.wait_ge(s_t2out, 16)

            @block.vector
            def _(dve):
                link = chain(dve, "s_epi1_chain")
                dve.wait_ge(s_part[2], 16)
                for c in range(1, K):
                    dve.wait_ge(s_part[c % 2], 16 * ((c + 1) // 2))
                    nv.tensor_tensor(flat_acc, flat_acc, parts[c % 2], ALU.add).then_inc(s_used, 1)
                    dve.wait_ge(s_used, c)
                tot = stat[:, 0, :]
                link(nv.tensor_scalar(tot, acc[:, 0:NB, C], 1e-8, None, ALU.max))
                link(nv.reciprocal(stat[:, 1, :], tot))
                link(nv.tensor_tensor(acc[:, 0:NB, 0:C], acc[:, 0:NB, 0:C], stat[:, 1, :].unsqueeze(2).to_broadcast([P, NB, C]), ALU.mult))
                link(nv.tensor_tensor(h[:, :, :], h[:, :, :], acc[:, 0:NB, 0:C], ALU.add))
                layernorm_relu(link, nv, None, s_var2, s_std2, 0, h[:, :, :], acc[:, 0:NB, 0:C], gammab[:, :], betab[:, :])
                link(nv.tensor_tensor(nodes[:, :, :], nodes[:, :, :], acc[:, 0:NB, 0:C], ALU.add))
                layernorm_relu(link, nv, None, s_var2, s_std2, 1, nodes[:, :, :], h[:, :, :])
                link(nv.memset(t2[:, :, C:CS], 1.0))
                nv.tensor_copy(t2[:, :, 0:C], h[:, :, :]).then_inc(s_t2, 1)

            @block.scalar
            def _(act):
                std(act, s_var2, s_std2, 0)
                std(act, s_var2, s_std2, 1)
                nc.scalar.activation(lg[:, :], lg[:, :], ACT.Exp).then_inc(s_exped, 1)

        spmm_pass(1, "l2", table2, CS, lg, False)

        def table_out(sp, s_made, s_landed, dram_table, src):
            sp.wait_ge(s_made, 1)
            sp.dma_start(dram_table.rearrange("(p b) c -> p (b c)", p=P), src).then_inc(s_landed, 16)
            sp.wait_ge(s_landed, 16)

        s_var3 = sem("s_var3"); s_std3 = sem("s_std3"); s_neg = sem("s_neg"); s_elu = sem("s_elu")
        s_h3 = sem("s_h3"); s_h3out = sem("s_h3out")
        e3 = scratch[:, 0:NB * C].rearrange("p (b c) -> p b c", c=C)
        with nc.Block() as block:
            @block.sync
            def _(sp):
                table_out(sp, s_h3, s_h3out, table3[0], h_flat)

            @block.vector
            def _(dve):
                link = chain(dve, "s_epi2_chain")
                a3 = acc[:, 0:NB, 0:C]
                link(nv.tensor_scalar(stat[:, 0, :], acc[:, 0:NB, C], 1e-30, None, ALU.max))
                link(nv.reciprocal(stat[:, 1, :], stat[:, 0, :]))
                link(nv.tensor_tensor(a3, a3, stat[:, 1, :].unsqueeze(2).to_broadcast([P, NB, C]), ALU.mult))
                nv.tensor_scalar(e3, a3, 0.0, None, ALU.min).then_inc(s_neg, 1)
                link(nv.tensor_scalar(a3, a3, 0.0, -1.0, ALU.max, ALU.add))
                link(nv.tensor_tensor(nodes[:, :, :], nodes[:, :, :], a3, ALU.add))
                dve.wait_ge(s_elu, 1)
                link(nv.tensor_tensor(nodes[:, :, :], nodes[:, :, :], e3, ALU.add))
                layernorm_relu(link, nv, None, s_var3, s_std3, 0, nodes[:, :, :], h[:, :, :])
                nv.memset(stat[:, 0, 0:1], 0.0).then_inc(s_h3, 1)

            @block.scalar
            def _(act):
                act.wait_ge(s_neg, 1)
                nc.scalar.activation(scratch[:, 0:NB * C], scratch[:, 0:NB * C], ACT.Exp).then_inc(s_elu, 1)
                std(act, s_var3, s_std3, 0)

        spmm_pass(2, "l3a", table3[0], C, w, False)
        s_y1 = sem("s_y1"); s_y1out = sem("s_y1out")
        third = 1.0 / (LAYERS + 1)
        with nc.Block() as block:
            @block.sync
            def _(sp):
                table_out(sp, s_y1, s_y1out, table3[1], scratch[:, 0:NB * C])

            @block.vector
            def _(dve):
                link = chain(dve, "s_epi3_chain")
                nv.tensor_copy(e3, acc[:, 0:NB, 0:C]).then_inc(s_y1, 1)
                link(nv.tensor_tensor(h[:, :, :], h[:, :, :], acc[:, 0:NB, 0:C], ALU.add))
                link(nv.scalar_tensor_tensor(out=nodes[:, :, :], in0=h[:, :, :], scalar=third, in1=nodes[:, :, :], op0=ALU.mult, op1=ALU.add))

        spmm_pass(3, "l3b", table3[1], C, w, False)
        s_res = sem("s_res"); s_resout = sem("s_resout")
        with nc.Block() as block:
            @block.vector
            def _(dve):
                nv.scalar_tensor_tensor(out=nodes[:, :, :], in0=acc[:, 0:NB, 0:C], scalar=third, in1=nodes[:, :, :],
                                        op0=ALU.mult, op1=ALU.add).then_inc(s_res, 1)

            @block.sync
            def _(sp):
                sp.wait_ge(s_res, 1)
                sp.dma_start(out, nodes[:, :, :].rearrange("p b c -> p (b c)")).then_inc(s_resout, 16)
                sp.wait_ge(s_resout, 16)


def kernel(x, src, dst, edge_attr_40, edge_weight, edge_weight1, node_type_119, node_vec, L1_gnn_W1, L1_gnn_b1,
           L1_gnn_W2, L1_gnn_b2, L1_gnn_emb, L1_gnn_adaptW, L1_gnn_gamma, L1_gnn_beta):
    import numpy as np
    import concourse.bacc as bacc
    from concourse.bass_utils import run_bass_kernel_spmd

    def padded(a, n, fill=0):
        a = np.asarray(a)
        return np.concatenate([a, np.full((n - a.shape[0],) + a.shape[1:], fill, a.dtype)])

    def node_major(a):
        a = padded(a, NPAD)
        a = a.reshape(NB, P, -1).transpose(1, 0, 2)
        return a.reshape(P, -1)

    ne = T * P
    last = NPAD - 1
    s, d = padded(src, ne, last), padded(dst, ne, last)
    ew, lgt = padded(edge_weight, ne), padded(np.asarray(edge_weight1)[:, 0], ne)
    arrays = {
        "x": node_major(x),
        "dst_cols": d.reshape(T, P).T, "src_cols": s.reshape(T, P).T,
        "dst_rows": d.reshape(NG, GW), "src_rows": s.reshape(NG, GW),
        "w_cols": ew.reshape(T, P).T, "logit_cols": lgt.reshape(T, P).T, "logit_rows": lgt.reshape(NG, GW),
        "attr_t": padded(edge_attr_40, ne).T,
        "type_row": padded(node_type_119, NPAD).reshape(1, NPAD),
        "mult": node_major(node_vec),
        "w1_t": np.asarray(L1_gnn_W1).T, "b1": np.asarray(L1_gnn_b1).reshape(C, 1),
        "w2e": np.concatenate([np.asarray(L1_gnn_W2).T, np.asarray(L1_gnn_b2).reshape(1, C)]),
        "emb": np.asarray(L1_gnn_emb), "emb_t": np.asarray(L1_gnn_emb).T, "adapt_t": np.asarray(L1_gnn_adaptW).T,
        "gamma": np.asarray(L1_gnn_gamma), "beta": np.asarray(L1_gnn_beta),
    }
    arrays = {f"in_{k}": np.ascontiguousarray(v) for k, v in arrays.items()}
    nc = bacc.Bacc("TRN2", target_bir_lowering=False, num_devices=1)
    args = [nc.dram_tensor(k, v.shape, mybir.dt.from_np(v.dtype), kind="ExternalInput").ap() for k, v in arrays.items()]
    out = nc.dram_tensor("out", (P, NB * C), mybir.dt.float32, kind="ExternalOutput").ap()
    gnn_kernel(nc, *args, out)
    r = run_bass_kernel_spmd(nc, [arrays], core_ids=[0])
    y = np.asarray(r.results[0]["out"]).reshape(P, NB, C).transpose(1, 0, 2).reshape(NPAD, C)
    return np.ascontiguousarray(y[:N])
```

```python
import concourse.bass as bass
from concourse import mybir
from contextlib import ExitStack

N = 12500
C = 48
E = 212500
R = 40
NEL = 119
GE = 32
P = 128
NB_BITS = 7
NB = -(-N // P)
NPAD = NB * P
NBW = NB + 2
G = 4
GB = 4
U = G * GB
NG = -(-E // (P * U)) * GB
T = NG * G
TURNS = NG // GB
GW = G * P
AHEAD = 3
TI = T + AHEAD * G
PARTS = 3
WB = 2
C0 = C + GE
CS = C + 1
CT = C + 2
K = 8
TRASH = NPAD
NR = NPAD + P
CUTOFF = 6.0
LN_EPS = 1e-5
BIG = 1e30
LAYERS = 2
ZB = 7
PI = 3.141592653589793


def gnn_kernel(nc, x, dst_cols, src_cols, dst_rows, src_rows, w_cols, logit_cols, logit_rows,
               attr_t, type_row, mult, w1_t, b1, w2e, emb, emb_t, adapt_t, gamma, beta, out):
    f32 = mybir.dt.float32
    i32 = mybir.dt.int32
    u16 = mybir.dt.uint16
    bf16 = mybir.dt.bfloat16
    ALU = mybir.AluOpType
    ACT = mybir.ActivationFunctionType
    X_AXIS = mybir.AxisListType.X
    ds = bass.ds

    with ExitStack() as ctx:
        def sb(name, shape, dt=f32):
            return ctx.enter_context(nc.sbuf_tensor(name, shape, dt))

        def sem(name):
            return ctx.enter_context(nc.semaphore(name))

        def dram(name, shape, dt=f32):
            return nc.dram_tensor(name, shape, dt, kind="Internal").ap()

        table0 = dram("table0", (NPAD, C0))
        table2 = dram("table2", (NPAD, CS))
        table3 = [dram(f"table3_{k}", (NPAD, C)) for k in range(LAYERS)]
        sums = [dram(f"sums{k}", (NR, CS)) for k in range(K)]
        rows16_dram = dram("rows16_dram", (2, NG, GW), u16)
        ranges_dram = dram("ranges_dram", (TURNS, GB * 2), i32)

        nodes = sb("nodes", [P, NB, C])
        h = sb("h", [P, NB, C])
        acc = sb("acc", [P, NBW, CS])
        table = sb("table", [P, NBW, PARTS, CT], bf16)
        embq = table[:, :, :, :].rearrange("p b k c -> p (b k c)")[:, 0:NBW * PARTS * GE].rearrange("p (b k c) -> p b k c", k=PARTS, c=GE)
        scratch = sb("scratch", [P, NB * CS + 16])
        iota = sb("iota", [P, NBW * P], u16)
        dstf = sb("dstf", [P, TI])
        w = sb("w", [P, TI])
        cw = sb("cw", [P, T])
        lg = sb("lg", [P, TI])
        adapt = sb("adapt", [P, T])
        srow = sb("srow", [P, TI])
        ranges = sb("ranges", [1, NG * 2], i32)
        node = sb("node", [P, NBW])
        segmax = sb("segmax", [P, NBW])
        multc = sb("multc", [P, NB])
        gammab = sb("gammab", [P, C])
        betab = sb("betab", [P, C])
        w1s = sb("w1s", [R, C])
        b1s = sb("b1s", [C, 1])
        w2s = sb("w2s", [C + 1, C])
        lower = sb("lower", [P, P], bf16)
        trash = sb("trash", [P, 1])
        zeros = sb("zeros", [1, G * CT], bf16)
        idx = sb("idx", [P, U], i32)
        rows = sb("rows", [P, U, C0])
        onehot = sb("onehot", [P, G, WB * P], bf16)
        onet = sb("onet", [P, WB, GW], bf16)
        same = sb("same", [P, 2, G, P], bf16)
        drow = sb("drow", [P, 2, GW], u16)
        srcrow = sb("srcrow", [P, 2, GW], u16)
        lrow = sb("lrow", [P, 2, GW])
        attr = lrow[0:R, :, :]
        hid = sb("hid", [C + 1, 2, GW])
        gate = sb("gate", [P, G, CS])
        prod = sb("prod", [P, 2, G, CS])
        rest = sb("rest", [P, G, CS])
        parts = sb("parts", [P, 2, G, PARTS, CS], bf16)
        dup = sb("dup", [P, G])
        dmp = sb("dmp", [P, G])
        wmax = sb("wmax", [P, WB])
        dots = sb("dots", [P, G, GE])
        pen = scratch[:, 0:WB * GW].rearrange("p (b e) -> p b e", b=WB)
        junk = scratch[:, WB * GW:2 * WB * GW].rearrange("p (b e) -> p b e", b=WB)
        def ps(name, shape):
            return ctx.enter_context(nc.psum_tensor(name, shape, f32))

        psum_acc = ps("psum_acc", [P, WB, 512])
        psum_exp = [ps(f"psum_exp{r}", [P, 512]) for r in range(2)]
        psum_gate = ps("psum_gate", [P, 512])
        psum_comb = [ps(f"psum_comb{r}", [P, 512]) for r in range(2)]
        psum_hid = ps("psum_hid", [P, 512])

        zc = scratch[0:NEL, 0:2 * ZB * P].bitcast(i32).rearrange("p (r n) -> p r n", r=2)
        zhot = scratch[0:NEL, 2 * ZB * P:4 * ZB * P].rearrange("p (r n) -> p r n", r=2)
        typec = sb("typec", [P, 1])
        ea = sb("ea", [NEL, 2 * GE])
        embts = sb("embts", [GE, NEL])
        adapts = sb("adapts", [GE, GE])
        stat = sb("stat", [P, 4, NB])
        tbl_flat = table[:, :, :, :].rearrange("p b k c -> p (b k c)").bitcast(f32)
        acc_flat = acc[:, :, :].rearrange("p b c -> p (b c)")
        h_flat = h[:, :, :].rearrange("p b c -> p (b c)")
        int_a = tbl_flat[:, 0:T].bitcast(i32)
        int_b = tbl_flat[:, T:2 * T].bitcast(i32)
        int_c = tbl_flat[:, 2 * T:3 * T].bitcast(i32)
        embst = acc_flat[:, 0:NB * GE].rearrange("p (b c) -> p b c", c=GE)
        embq32 = h_flat[:, 0:NB * GE].rearrange("p (b c) -> p b c", c=GE)
        dr_i = h_flat[0:TURNS, 0:GB * GW].bitcast(i32)
        sr_i = h_flat[0:TURNS, GB * GW:2 * GB * GW].bitcast(i32)
        rows16 = scratch[0:TURNS, GB * GW:2 * GB * GW].bitcast(u16).rearrange("q (k e) -> q k e", k=2)
        wk_i = stat[:, :, :].rearrange("p a b -> p (a b)").bitcast(i32)

        def by_partition(t, c):
            return t.rearrange("(p b) c -> p b c", p=P)[:, :, c[0]:c[1]]

        def layernorm_relu(link, nv, na, s_var, s_std, turn, src, dst, mul=None, add=None):
            d3 = scratch[:, 0:NB * C].rearrange("p (b c) -> p b c", c=C)
            s, v, r = stat[:, 0, :], stat[:, 1, :], stat[:, 2, :]
            bc = lambda a: a.unsqueeze(2).to_broadcast([P, NB, C])
            link(nv.tensor_reduce(out=s, in_=src, axis=X_AXIS, op=ALU.add))
            link(nv.tensor_scalar(s, s, 1.0 / C, None, ALU.mult))
            link(nv.tensor_tensor(dst, src, bc(s), ALU.subtract))
            link(nv.tensor_tensor(d3, dst, dst, ALU.mult))
            link(nv.tensor_reduce(out=v, in_=d3, axis=X_AXIS, op=ALU.add))
            nv.tensor_scalar(v, v, 1.0 / C, LN_EPS, ALU.mult, ALU.add).then_inc(s_var, 1)
            nv.wait_ge(s_std, turn + 1)
            link(nv.reciprocal(r, stat[:, 3, :]))
            if mul is None:
                link(nv.scalar_tensor_tensor(out=dst, in0=dst, scalar=0.0, in1=bc(r), op0=ALU.max, op1=ALU.mult))
            else:
                link(nv.tensor_tensor(dst, dst, bc(r), ALU.mult))
                link(nv.tensor_tensor(dst, dst, mul.unsqueeze(1).to_broadcast([P, NB, C]), ALU.mult))
                link(nv.tensor_tensor(dst, dst, add.unsqueeze(1).to_broadcast([P, NB, C]), ALU.add))

        def split(link, to, x, left):
            link(nv.tensor_copy(to[:, :, 0, :], x))
            link(nv.tensor_tensor(left, x, to[:, :, 0, :], ALU.subtract))
            link(nv.tensor_copy(to[:, :, 1, :], left))
            link(nv.tensor_tensor(to[:, :, 2, :], left, to[:, :, 1, :], ALU.subtract))

        def std(act, s_var, s_std, turn):
            act.wait_ge(s_var, turn + 1)
            nc.scalar.activation(stat[:, 3, :], stat[:, 1, :], ACT.Sqrt).then_inc(s_std, 1)

        def chain(eng, name):
            s, n = sem(name), [0]

            def link(instruction):
                n[0] += 1
                instruction.then_inc(s, 1)
                eng.wait_ge(s, n[0])
            return link

        nv = nc.vector

        s_x = sem("s_x"); s_ints = sem("s_ints"); s_rowints = sem("s_rowints"); s_w = sem("s_w")
        s_lg = sem("s_lg"); s_small = sem("s_small"); s_consts = sem("s_consts")
        s_srowd = sem("s_srowd"); s_srowout = sem("s_srowout"); s_ranged = sem("s_ranged")
        s_rangeout = sem("s_rangeout"); s_rangein = sem("s_rangein")
        s_zin = [sem(f"s_zin{r}") for r in range(2)]
        s_zhot = sem("s_zhot"); s_zmm = sem("s_zmm"); s_zout = sem("s_zout")
        s_ea = sem("s_ea"); s_eamm = sem("s_eamm")
        s_var = sem("s_var"); s_std = sem("s_std")
        s_h0 = sem("s_h0"); s_table0 = sem("s_table0"); s_sin = sem("s_sin"); s_sinin = sem("s_sinin")
        s_zero = sem("s_zero"); s_cleared = sem("s_cleared")
        ZT = NB // ZB
        with nc.Block() as block:
            @block.sync
            def _(sp):
                sp.dma_start(int_a, src_cols).then_inc(s_ints, 16)
                sp.dma_start(int_b, dst_cols).then_inc(s_ints, 16)
                sp.dma_start(dr_i, dst_rows.rearrange("(q j) e -> q (j e)", j=GB)).then_inc(s_rowints, 16)
                sp.dma_start(sr_i, src_rows.rearrange("(q j) e -> q (j e)", j=GB)).then_inc(s_rowints, 16)
                sp.dma_start(w[:, 0:T], w_cols).then_inc(s_w, 16)
                sp.dma_start(nodes[:, :, :].rearrange("p b c -> p (b c)"), x).then_inc(s_x, 16)
                sp.dma_start(lg[:, 0:T], logit_cols).then_inc(s_lg, 16)
                sp.wait_ge(s_srowd, 1)
                for k in range(2):
                    sp.dma_start(rows16_dram[k].rearrange("(q j) e -> q (j e)", j=GB), rows16[:, k, :]).then_inc(s_srowout, 16)
                sp.wait_ge(s_ranged, 1)
                sp.dma_start(ranges_dram, idx[0:TURNS, 0:2 * GB]).then_inc(s_rangeout, 16)
                sp.wait_ge(s_rangeout, 16)
                sp.dma_start(ranges[0:1, :], ranges_dram.rearrange("q j -> (q j)").unsqueeze(0)).then_inc(s_rangein, 16)
                sp.wait_ge(s_rangein, 16)
                sp.wait_ge(s_srowout, 32)
                sp.wait_ge(s_lg, 16)

            @block.gpsimd
            def _(pool):
                nc.gpsimd.iota(iota[:, :], pattern=[[1, NBW * P]], base=0, channel_multiplier=0).then_inc(s_consts, 1)
                nc.gpsimd.memset(lower[:, :], 1.0).then_inc(s_consts, 1)
                pool.wait_ge(s_consts, 2)
                nc.gpsimd.affine_select(out=lower[:, :], in_=lower[:, :], compare_op=ALU.is_gt, fill=0.0,
                                        base=0, pattern=[[-1, P]], channel_multiplier=1).then_inc(s_consts, 1)

            @block.scalar
            def _(act):
                act.dma_start(multc[:, :], mult).then_inc(s_small, 16)
                act.dma_start(gammab[:, :], gamma.partition_broadcast(P)).then_inc(s_small, 16)
                act.dma_start(betab[:, :], beta.partition_broadcast(P)).then_inc(s_small, 16)
                act.dma_start(w1s[:, :], w1_t).then_inc(s_small, 16)
                act.dma_start(b1s[:, :], b1).then_inc(s_small, 16)
                act.dma_start(w2s[:, :], w2e).then_inc(s_small, 16)
                act.dma_start(ea[:, 0:GE], emb).then_inc(s_small, 16)
                act.dma_start(embts[:, :], emb_t).then_inc(s_small, 16)
                act.dma_start(adapts[:, :], adapt_t).then_inc(s_small, 16)
                act.wait_ge(s_small, 9 * 16)

            @block.vector
            def _(dve):
                link = chain(dve, "s_setup_chain")
                nv.memset(zeros[:, :], 0.0)
                nv.memset(acc_flat, 0.0)
                nv.memset(segmax[:, :], -BIG)
                for columns in (srow, dstf, w, lg):
                    nv.memset(columns[:, T:TI], 0.0)
                nv.memset(hid[:, :, :], 1.0)
                nv.memset(gate[:, :, :], 1.0)
                dve.wait_ge(s_ints, 32)
                nv.tensor_copy(dstf[:, 0:T], int_b)
                link(nv.tensor_scalar(int_c, int_a, NB_BITS, None, ALU.logical_shift_right))
                link(nv.tensor_scalar(int_a, int_a, P - 1, None, ALU.bitwise_and))
                link(nv.scalar_tensor_tensor(out=srow[:, 0:T], in0=int_a, scalar=float(NB), in1=int_c, op0=ALU.mult, op1=ALU.add))
                dve.wait_ge(s_rowints, 32)
                tmp = scratch[0:TURNS, 0:GB * GW].bitcast(i32)
                link(nv.tensor_scalar(tmp, sr_i, NB_BITS, None, ALU.logical_shift_right))
                link(nv.tensor_scalar(sr_i, sr_i, P - 1, None, ALU.bitwise_and))
                nv.tensor_copy(rows16[:, 0, :], dr_i)
                nv.scalar_tensor_tensor(out=rows16[:, 1, :], in0=sr_i, scalar=float(NB),
                                        in1=tmp, op0=ALU.mult, op1=ALU.add).then_inc(s_srowd, 1)
                d4 = dr_i.rearrange("q (j e) -> q j e", j=GB)
                lo = wk_i[0:TURNS, 0:GB]
                hi = wk_i[0:TURNS, GB:2 * GB]
                link(nv.tensor_reduce(out=lo, in_=d4, axis=X_AXIS, op=ALU.min))
                link(nv.tensor_reduce(out=hi, in_=d4, axis=X_AXIS, op=ALU.max))
                link(nv.tensor_scalar(lo, lo, NB_BITS, None, ALU.logical_shift_right))
                link(nv.tensor_scalar(hi, hi, NB_BITS, None, ALU.logical_shift_right))
                pairs = idx[0:TURNS, 0:2 * GB].rearrange("q (j k) -> q j k", k=2)
                link(nv.tensor_copy(pairs[:, :, 0], lo))
                link(nv.tensor_scalar(pairs[:, :, 1], hi, 1.0, None, ALU.add))
                nv.memset(stat[:, 3, 1:2], 0.0).then_inc(s_ranged, 1)

        with nc.Block() as block:
            @block.sync
            def _(sp):
                for c in range(K):
                    sp.dma_start(sums[c].rearrange("(p r) c -> p (r c)", p=P), acc_flat[:, 0:NR // P * CS]).then_inc(s_cleared, 16)
                sp.wait_ge(s_cleared, 16 * K)

            @block.gpsimd
            def _(pool):
                nc.gpsimd.iota(int_a[:, 0:1], pattern=[[0, 1]], base=0, channel_multiplier=1).then_inc(s_consts, 1)
                nc.gpsimd.iota(int_a[:, 1:1 + NBW], pattern=[[P, NBW]], base=0, channel_multiplier=1).then_inc(s_consts, 1)
                nc.gpsimd.iota(int_a[:, 1 + NBW:2 + NBW], pattern=[[0, 1]], base=TRASH, channel_multiplier=1).then_inc(s_consts, 1)

            @block.vector
            def _(dve):
                link = chain(dve, "s_const_chain")
                dve.wait_ge(s_consts, 6)
                link(nv.tensor_copy(typec[:, :], int_a[:, 0:1]))
                link(nv.tensor_copy(node[:, :], int_a[:, 1:1 + NBW]))
                link(nv.tensor_copy(trash[:, :], int_a[:, 1 + NBW:2 + NBW]))
                a, b = int_c.bitcast(f32), int_b
                k12 = 2 * CUTOFF
                link(nv.tensor_scalar(a, w[:, 0:T], -1.0, None, ALU.mult))
                link(nv.tensor_tensor(a, a, w[:, 0:T], ALU.max))
                link(nv.tensor_scalar(b, a, 1.0 / k12, None, ALU.mult))
                link(nv.scalar_tensor_tensor(out=a, in0=b, scalar=-k12, in1=a, op0=ALU.mult, op1=ALU.add))
                c = cw[:, :]
                link(nv.tensor_scalar(c, a, -1.0, None, ALU.mult))
                link(nv.tensor_tensor(a, a, c, ALU.max))
                link(nv.tensor_scalar(c, a, -1.0, k12, ALU.mult, ALU.add))
                link(nv.tensor_tensor(a, a, c, ALU.min))
                nv.tensor_scalar(a, a, -PI / CUTOFF, PI / 2, ALU.mult, ALU.add).then_inc(s_sinin, 1)
                dve.wait_ge(s_sin, 1)
                link(nv.tensor_scalar(c, c, 0.5, 0.5, ALU.mult, ALU.add))
                link(nv.scalar_tensor_tensor(out=c, in0=w[:, 0:T], scalar=CUTOFF, in1=c, op0=ALU.is_lt, op1=ALU.mult))
                dve.wait_ge(s_eamm, 1)
                nv.tensor_copy(ea[:, GE:2 * GE], psum_gate[0:NEL, 0:GE]).then_inc(s_ea, 1)
                for q in range(ZT):
                    dve.wait_ge(s_zin[q % 2], 16 * (q // 2 + 1))
                    if q >= 2:
                        dve.wait_ge(s_zmm, q - 1)
                    nv.tensor_scalar(zhot[:, q % 2, :], zc[:, q % 2, :], typec[0:NEL, 0:1], None,
                                     ALU.is_equal).then_inc(s_zhot, 1)
                dve.wait_ge(s_zout, ZT)
                link(nv.memset(embq[:, NB:NBW, :, :], 0.0))
                split(link, embq[:, 0:NB, :, :], embq32, scratch[:, 0:NB * GE].rearrange("p (b c) -> p b c", c=GE))
                layernorm_relu(link, nv, None, s_var, s_std, 0, nodes[:, :, :], h[:, :, :])
                nv.memset(stat[:, 0, 0:1], 0.0).then_inc(s_h0, 1)

            @block.tensor
            def _(pe):
                nc.tensor.matmul(psum_gate[0:NEL, 0:GE], embts[:, :], adapts[:, :], start=True, stop=True).then_inc(s_eamm, 1)
                pe.wait_ge(s_ea, 1)
                for q in range(ZT):
                    pe.wait_ge(s_zhot, q + 1)
                    if q >= 2:
                        pe.wait_ge(s_zout, q - 1)
                    for b in range(ZB):
                        last = nc.tensor.matmul(psum_exp[q % 2][:, b * 2 * GE:(b + 1) * 2 * GE],
                                                zhot[:, q % 2, b * P:(b + 1) * P], ea[:, :], start=True, stop=True)
                    last.then_inc(s_zmm, 1)

            @block.scalar
            def _(act):
                act.wait_ge(s_sinin, 1)
                nc.scalar.activation(cw[:, :], int_c.bitcast(f32), ACT.Sin).then_inc(s_sin, 1)
                for q in range(min(2, ZT)):
                    act.dma_start(zc[:, q, :], type_row[0, q * ZB * P:(q + 1) * ZB * P].partition_broadcast(NEL)).then_inc(s_zin[q], 16)
                act.wait_ge(s_cleared, 16 * K)
                for q in range(ZT):
                    act.wait_ge(s_zmm, q + 1)
                    pv = psum_exp[q % 2][:, 0:ZB * 2 * GE].rearrange("p (b c) -> p b c", c=2 * GE)
                    nc.scalar.copy(embst[:, q * ZB:(q + 1) * ZB, :], pv[:, :, 0:GE])
                    nc.scalar.copy(embq32[:, q * ZB:(q + 1) * ZB, :], pv[:, :, GE:2 * GE]).then_inc(s_zout, 1)
                    if q + 2 < ZT:
                        act.dma_start(zc[:, q % 2, :], type_row[0, (q + 2) * ZB * P:(q + 3) * ZB * P].partition_broadcast(NEL)).then_inc(s_zin[q % 2], 16)
                act.wait_ge(s_zout, ZT)
                act.dma_start(by_partition(table0, (C, C0)), embst).then_inc(s_table0, 16)
                std(act, s_var, s_std, 0)
                act.wait_ge(s_h0, 1)
                act.dma_start(by_partition(table0, (0, C)), h[:, :, :]).then_inc(s_table0, 16)
                act.wait_ge(s_table0, 32)

        s_rows = [sem(f"s_rows{j}") for j in range(GB)]
        s_prod32 = sem("s_prod32")
        s_part0 = sem("s_part0")
        s_rest = sem("s_rest")
        s_part1 = sem("s_part1")
        s_part2 = sem("s_part2")
        s_hot = [sem(f"s_hot{u}") for u in range(G)]
        s_mm = sem("s_mm")
        s_added = sem("s_added")
        s_onet = sem("s_onet")
        s_exp = sem("s_exp")
        s_pen = sem("s_pen")
        s_wmax = sem("s_wmax")
        s_maxed = sem("s_maxed")
        s_closed = sem("s_closed")
        s_dots = sem("s_dots")
        s_seen = sem("s_seen")
        wn_dve = nc.vector.alloc_register("dve_window")
        wn_pe = nc.tensor.alloc_register("pe_window")
        wn_act = nc.scalar.alloc_register("act_window")
        range_regs = {e: [e.alloc_register(f"range{k}_{n}") for k in range(2 * GB)]
                      for n, e in (("dve", nc.vector), ("pe", nc.tensor), ("act", nc.scalar))}

        def load_ranges(eng, i):
            regs = range_regs[eng]
            eng.load(regs, ranges[0:1, ds(i * (2 * GB), 2 * GB)])
            return [(eng.snap(regs[2 * j], min_val=0, max_val=NB - 1), eng.snap(regs[2 * j + 1], min_val=1, max_val=NB))
                    for j in range(GB)]

        def spmm_pass(order, name, src_table, cols, weights, first):
            s_idx = sem(name + "_idx")
            s_free = sem(name + "_free")
            s_clear = sem(name + "_clear")
            s_bcast = [sem(f"{name}_bcast{r}") for r in range(2)] if first else None
            width = src_table.shape[1]
            past = order * (NG + 1)
            passed = order * NG

            with nc.Block() as block:
                @block.gpsimd
                def _(pool):
                    def gather(g, j):
                        pool.wait_ge(s_idx, g + 1)
                        pool.sem_inc(s_seen, 1)
                        for u in range(j * G, (j + 1) * G):
                            pool.indirect_dma_start(
                                out=rows[:, u, 0:width], out_offset=None, in_=src_table,
                                in_offset=bass.IndirectOffsetOnAxis(ap=idx[:, u:u + 1], axis=0)).then_inc(s_rows[j], 16)

                    with pool.Fori(0, TURNS) as i:
                        for j in range(GB):
                            gather(i * GB + j, j)
                    gather(NG, 0)

                if first:
                    @block.sync
                    def _(sp):
                        with sp.Fori(0, TURNS) as i:
                            for j in range(GB):
                                sp.wait_ge(s_free, i * GB + (j + GB - 1))
                                sp.dma_start(drow[:, j % 2, :], rows16_dram[0, ds(i * GB + j, 1), :].squeeze(0).partition_broadcast(P)).then_inc(s_bcast[j % 2], 16)
                                sp.dma_start(lrow[:, j % 2, :], logit_rows[ds(i * GB + j, 1), :].squeeze(0).partition_broadcast(P)).then_inc(s_bcast[j % 2], 16)

                @block.scalar
                def _(act):
                    def stage(slot, column):
                        nc.scalar.copy(idx[:, slot * G:(slot + 1) * G], srow[:, ds(column, G)]).then_inc(s_idx, 1)

                    def part0(g, par):
                        act.wait_ge(s_prod32, g + (past + 1))
                        act.sem_inc(s_seen, 1)
                        nc.scalar.copy(parts[:, par, :, 0, 0:cols], prod[:, par, :, 0:cols]).then_inc(s_part0, 1)

                    def part1(g, par):
                        act.wait_ge(s_rest, g + (past + 1))
                        act.sem_inc(s_seen, 1)
                        nc.scalar.copy(parts[:, par, :, 1, 0:cols], rest[:, :, 0:cols]).then_inc(s_part1, 1)

                    for j in range(AHEAD):
                        stage(j, j * G)
                    if first:
                        act.reg_mov(wn_act, 1)
                    part0(0, 0)
                    part1(0, 0)
                    with act.Fori(0, TURNS) as i:
                        spans = load_ranges(act, i) if first else None
                        for j in range(GB):
                            act.wait_ge(s_free, i * GB + (j + GB))
                            act.sem_inc(s_seen, 1)
                            stage((j + AHEAD) % GB, i * U + (j + AHEAD) * G)
                            part0(i * GB + (j + 1), (j + 1) % 2)
                            if first:
                                with act.Fori(*spans[j], WB) as k:
                                    win = act.snap(wn_act)
                                    act.wait_ge(s_wmax, win * WB)
                                    act.sem_inc(s_seen, 1)
                                    act.wait_ge(s_onet, win)
                                    nc.scalar.activation(pen, onet[:, :, :], ACT.Copy, scale=BIG, bias=-BIG).then_inc(s_pen, 1)
                                    act.reg_add(wn_act, wn_act, 1)
                            part1(i * GB + (j + 1), (j + 1) % 2)

                @block.vector
                def _(dve):
                    nv.memset(acc_flat, 0.0).then_inc(s_clear, 1)
                    dve.wait_ge(s_clear, 1)
                    dve.sem_inc(s_free, GB)
                    if first:
                        dve.sem_inc(s_added, 1)
                        dve.sem_inc(s_exp, 1)
                        dve.sem_inc(s_wmax, WB)
                        dve.sem_inc(s_maxed, 1)
                        dve.reg_mov(wn_dve, 1)

                    def weigh(i, j):
                        q = i + 1 if j == GB else i
                        dve.wait_ge(s_rows[j % GB], q * (16 * G) + (order * (TURNS + (j % GB == 0)) + 1) * 16 * G)
                        last = nv.tensor_tensor(prod[:, j % 2, :, 0:cols], rows[:, (j % GB) * G:(j % GB + 1) * G, 0:cols],
                                                weights[:, ds(i * U + j * G, G)].unsqueeze(2).to_broadcast([P, G, cols]), ALU.mult)
                        last.then_inc(s_prod32, 1)

                    def leave(g, par):
                        dve.wait_ge(s_part0, g + (past + 1))
                        nv.tensor_tensor(rest[:, :, 0:cols], prod[:, par, :, 0:cols], parts[:, par, :, 0, 0:cols], ALU.subtract).then_inc(s_rest, 1)

                    def part2(g, par):
                        dve.wait_ge(s_part1, g + (past + 1))
                        nv.tensor_tensor(parts[:, par, :, 2, 0:cols], rest[:, :, 0:cols], parts[:, par, :, 1, 0:cols], ALU.subtract).then_inc(s_part2, 1)

                    weigh(0, 0)
                    leave(0, 0)
                    with dve.Fori(0, TURNS) as i:
                        spans = load_ranges(dve, i)
                        for j in range(GB):
                            g = i * GB + j
                            weigh(i, j + 1)
                            if not first:
                                dve.sem_inc(s_free, 1)
                            part2(g, j % 2)
                            if first:
                                dve.wait_ge(s_bcast[j % 2], i * (16 * GB) + 32 * (j // 2 + 1))
                                dve.sem_inc(s_seen, 1)
                            with dve.Fori(*spans[j], WB) as k:
                                win = dve.snap(wn_dve)
                                if first:
                                    dve.wait_ge(s_exp, win)
                                    dve.sem_inc(s_seen, 1)
                                    for b in range(WB):
                                        last = nv.tensor_scalar(onet[:, b, :], drow[:, j % 2, :], node[:, ds(k + b, 1)], None, ALU.is_equal)
                                    last.then_inc(s_onet, 1)
                                for u in range(G):
                                    nv.tensor_scalar(onehot[:, u, :], iota[:, ds(k * P, WB * P)], dstf[:, ds(i * U + (j * G + u), 1)],
                                                     None, ALU.is_equal).then_inc(s_hot[u], 1)
                                if first:
                                    dve.wait_ge(s_pen, win)
                                    dve.sem_inc(s_seen, 1)
                                    for b in range(WB):
                                        nv.tensor_tensor_reduce(out=junk[:, b, :], in0=pen[:, b, :], in1=lrow[:, j % 2, :], scale=1.0,
                                                                scalar=-BIG, op0=ALU.add, op1=ALU.max,
                                                                accum_out=wmax[:, b:b + 1]).then_inc(s_wmax, 1)
                                    dve.wait_ge(s_maxed, win)
                                    dve.wait_ge(s_wmax, win * WB + WB)
                                    nv.tensor_tensor(segmax[:, ds(k, WB)], segmax[:, ds(k, WB)], wmax[:, :],
                                                     ALU.max).then_inc(s_maxed, 1)
                                dve.wait_ge(s_added, win)
                                dve.wait_ge(s_mm, win)
                                nv.tensor_tensor(acc[:, ds(k, WB), 0:cols], acc[:, ds(k, WB), 0:cols],
                                                 psum_acc[:, :, 0:cols], ALU.add).then_inc(s_added, 1)
                                dve.reg_add(wn_dve, wn_dve, 1)
                            if first:
                                pq = psum_exp[j % 2][:, 0:G * GE].rearrange("p (g c) -> p g c", c=GE)
                                dve.wait_ge(s_closed, g + 1)
                                nv.tensor_tensor(dots[:, :, :], rows[:, j * G:(j + 1) * G, C:C0], pq, ALU.mult).then_inc(s_dots, 1)
                            leave(g + 1, (j + 1) % 2)
                            if first:
                                dve.wait_ge(s_dots, g + 1)
                                nv.tensor_reduce(out=adapt[:, ds(i * U + j * G, G)], in_=dots[:, :, :], axis=X_AXIS,
                                                 op=ALU.add).then_inc(s_free, 1)

                @block.tensor
                def _(pe):
                    if first:
                        pe.reg_mov(wn_pe, 1)
                    with pe.Fori(0, TURNS) as i:
                        spans = load_ranges(pe, i)
                        for j in range(GB):
                            g = i * GB + j
                            if first:
                                pe.wait_ge(s_free, g + (GB - 1))
                                nc.tensor.matmul(psum_exp[j % 2][:, 0:G * GE], zeros[0:1, 0:P], zeros[0:1, 0:G * GE],
                                                 start=True, stop=False)
                            pe.wait_ge(s_part2, g + (passed + 1))
                            pe.sem_inc(s_seen, 1)
                            with pe.Fori(*spans[j], WB) as k:
                                win = pe.snap(wn_pe)
                                if first:
                                    pe.wait_ge(s_onet, win)
                                    for u in range(G):
                                        for b in range(WB):
                                            for q in range(PARTS):
                                                last = nc.tensor.matmul(psum_exp[j % 2][:, u * GE:(u + 1) * GE], onet[:, b, u * P:(u + 1) * P],
                                                                        embq[:, ds(k + b, 1), q, :].rearrange("p b c -> p (b c)"),
                                                                        start=False, stop=False)
                                    last.then_inc(s_exp, 1)
                                for u in range(G):
                                    pe.wait_ge(s_hot[u], win)
                                    for b in range(WB):
                                        for q in range(PARTS):
                                            last = nc.tensor.matmul(psum_acc[:, b, 0:cols], onehot[:, u, b * P:(b + 1) * P],
                                                                    parts[:, j % 2, u, q, 0:cols], start=(u == 0 and q == 0),
                                                                    stop=(u == G - 1 and q == PARTS - 1))
                                last.then_inc(s_mm, 1)
                                pe.reg_add(wn_pe, wn_pe, 1)
                            if first:
                                nc.tensor.matmul(psum_exp[j % 2][:, 0:G * GE], zeros[0:1, 0:P], zeros[0:1, 0:G * GE],
                                                 start=False, stop=True).then_inc(s_closed, 1)

        spmm_pass(0, "l0", table0, C, w, True)

        s_var1 = sem("s_var1"); s_std1 = sem("s_std1")
        with nc.Block() as block:
            @block.vector
            def _(dve):
                link = chain(dve, "s_epi0_chain")
                link(nv.memset(table[:, NB:NBW, :, :], 0.0))
                link(nv.tensor_tensor(nodes[:, :, :], nodes[:, :, :], acc[:, 0:NB, 0:C], ALU.add))
                layernorm_relu(link, nv, None, s_var1, s_std1, 0, nodes[:, :, :], h[:, :, :])
                hm = scratch[:, 0:NB * C].rearrange("p (b c) -> p b c", c=C)
                link(nv.tensor_tensor(hm, h[:, :, :], multc[:, :].unsqueeze(2).to_broadcast([P, NB, C]), ALU.mult))
                left = acc[:, 0:NB, 0:C]
                split(link, table[:, 0:NB, :, 0:C], hm, left)
                split(link, table[:, 0:NB, :, C:C + 1], multc[:, :].unsqueeze(2), left[:, :, 0:1])
                split(link, table[:, 0:NB, :, C + 1:CT], segmax[:, 0:NB].unsqueeze(2), left[:, :, 0:1])

            @block.scalar
            def _(act):
                std(act, s_var1, s_std1, 0)

        s_in = [sem(f"l1_in{r}") for r in range(2)]
        s_same = sem("l1_same"); s_dup = sem("l1_dup"); s_dmp = sem("l1_dmp"); s_idx1 = sem("l1_idx")
        s_hid = sem("l1_hid"); s_silu = sem("l1_silu"); s_onet1 = sem("l1_onet")
        s_exp1 = sem("l1_exp")
        s_mlp = sem("l1_mlp"); s_gate = sem("l1_gate")
        s_msg = sem("l1_msg")
        s_p0 = sem("l1_p0"); s_r = sem("l1_r"); s_p1 = sem("l1_p1"); s_p2 = sem("l1_p2")
        s_comb = sem("l1_comb")
        s_out = sem("l1_out")
        s_scat = [sem(f"l1_scat{c}") for c in range(K)]
        s_landed = sem("l1_landed")
        wn1_dve = nc.vector.alloc_register("l1_dve_window")
        wn1_pe = nc.tensor.alloc_register("l1_pe_window")
        with nc.Block() as block:
            @block.sync
            def _(sp):
                with sp.Fori(0, TURNS) as i:
                    for j in range(GB):
                        sp.wait_ge(s_msg, i * GB + (j + 1))
                        g = i * GB + j
                        sp.dma_start(drow[:, j % 2, :], rows16_dram[0, ds(g, 1), :].squeeze(0).partition_broadcast(P)).then_inc(s_in[j % 2], 16)
                        sp.dma_start(srcrow[:, j % 2, :], rows16_dram[1, ds(g, 1), :].squeeze(0).partition_broadcast(P)).then_inc(s_in[j % 2], 16)
                        sp.dma_start(attr[:, j % 2, :], attr_t[:, ds(g * GW, GW)]).then_inc(s_in[j % 2], 16)

            def inputs_here(eng, i, j):
                eng.wait_ge(s_in[j % 2], i * (48 * GB // 2) + 48 * (j // 2 + 1))

            @block.vector
            def _(dve):
                dve.sem_inc(s_msg, 2)
                dve.sem_inc(s_exp1, 1)
                dve.reg_mov(wn1_dve, 1)

                def leave(g, par):
                    dve.wait_ge(s_p0, g + 1)
                    nv.tensor_tensor(rest[:, :, :], prod[:, par, :, :], parts[:, par, :, 0, :], ALU.subtract).then_inc(s_r, 1)

                def part2(g, par):
                    dve.wait_ge(s_p1, g + 1)
                    nv.tensor_tensor(parts[:, par, :, 2, :], rest[:, :, :], parts[:, par, :, 1, :], ALU.subtract).then_inc(s_p2, 1)

                def turn(i, peeled):
                    spans = load_ranges(dve, i)
                    for j in range(GB):
                        g = i * GB + j
                        behind = j > 0 or not peeled
                        inputs_here(dve, i, j)
                        dve.sem_inc(s_seen, 1)
                        with dve.Fori(*spans[j], WB) as k:
                            win = dve.snap(wn1_dve)
                            dve.wait_ge(s_exp1, win)
                            dve.sem_inc(s_seen, 1)
                            for b in range(WB):
                                last = nv.tensor_scalar(onet[:, b, :], drow[:, j % 2, :], node[:, ds(k + b, 1)], None, ALU.is_equal)
                            last.then_inc(s_onet1, 1)
                            dve.reg_add(wn1_dve, wn1_dve, 1)
                        if j >= 2 or not peeled:
                            dve.wait_ge(s_comb, g - 1)
                            dve.sem_inc(s_seen, 1)
                        for u in range(G):
                            nv.tensor_scalar(same[:, j % 2, u, :], srcrow[:, j % 2, u * P:(u + 1) * P],
                                             srow[:, ds(i * U + (j * G + u), 1)], None, ALU.is_equal).then_inc(s_same, 1)
                        if behind:
                            leave(g - 1, (j - 1) % 2)
                        dve.wait_ge(s_same, g * G + G)
                        dve.sem_inc(s_seen, 1)
                        for u in range(G):
                            nv.tensor_tensor_reduce(out=onehot[:, u, 0:P], in0=same[:, j % 2, u, :], in1=lower[:, :], scale=1.0, scalar=0.0,
                                                    op0=ALU.mult, op1=ALU.max, accum_out=dup[:, u:u + 1]).then_inc(s_dup, 1)
                        dve.wait_ge(s_mlp, g + 1)
                        for u in range(G):
                            t = i * U + (j * G + u)
                            nv.tensor_scalar(gate[:, u, 0:C], psum_gate[:, u * C:(u + 1) * C], adapt[:, ds(t, 1)],
                                             cw[:, ds(t, 1)], ALU.add, ALU.mult).then_inc(s_gate, 1)
                        dve.wait_ge(s_dup, g * G + G)
                        nv.scalar_tensor_tensor(out=dmp[:, :], in0=srow[:, ds(i * U + j * G, G)], scalar=trash[:, 0:1],
                                                in1=dup[:, :], op0=ALU.subtract, op1=ALU.mult).then_inc(s_dmp, 1)
                        if behind:
                            part2(g - 1, (j - 1) % 2)
                        ph = psum_exp[j % 2][:, 0:G * CT].rearrange("p (g c) -> p g c", c=CT)
                        nv.tensor_tensor(lg[:, ds(i * U + j * G, G)], lg[:, ds(i * U + j * G, G)], ph[:, :, C + 1], ALU.subtract)
                        dve.wait_ge(s_gate, g * G + G)
                        nv.tensor_tensor(prod[:, j % 2, :, :], gate[:, :, :], ph[:, :, 0:CS], ALU.mult).then_inc(s_msg, 1)
                        dve.wait_ge(s_dmp, g + 1)
                        dve.wait_ge(s_landed, g + (GB - 1))
                        nv.tensor_tensor(idx[:, j * G:(j + 1) * G], srow[:, ds(i * U + j * G, G)], dmp[:, :], ALU.subtract).then_inc(s_idx1, 1)

                turn(0, True)
                with dve.Fori(1, TURNS) as i:
                    turn(i, False)
                leave(NG - 1, (NG - 1) % 2)
                part2(NG - 1, (NG - 1) % 2)

            @block.tensor
            def _(pe):
                pe.reg_mov(wn1_pe, 1)

                def combine(g, par):
                    pe.wait_ge(s_p2, g + 1)
                    pe.sem_inc(s_seen, 1)
                    pe.wait_ge(s_out, g + 1)
                    for u in range(G):
                        for q in range(PARTS):
                            last = nc.tensor.matmul(psum_comb[par][:, u * CS:(u + 1) * CS], same[:, par, u, :], parts[:, par, u, q, :],
                                                    start=(q == 0), stop=(q == PARTS - 1))
                    last.then_inc(s_comb, 1)

                def turn(i, peeled):
                    spans = load_ranges(pe, i)
                    for j in range(GB):
                        g = i * GB + j
                        inputs_here(pe, i, j)
                        pe.sem_inc(s_seen, 1)
                        nc.tensor.matmul(psum_hid[0:C, :], w1s[:, :], attr[:, j % 2, :], start=True, stop=True).then_inc(s_hid, 1)
                        pe.wait_ge(s_msg, g + 1)
                        nc.tensor.matmul(psum_exp[j % 2][:, 0:G * CT], zeros[0:1, 0:P], zeros[0:1, 0:G * CT], start=True, stop=False)
                        with pe.Fori(*spans[j], WB) as k:
                            win = pe.snap(wn1_pe)
                            pe.wait_ge(s_onet1, win)
                            for u in range(G):
                                for b in range(WB):
                                    for q in range(PARTS):
                                        last = nc.tensor.matmul(psum_exp[j % 2][:, u * CT:(u + 1) * CT], onet[:, b, u * P:(u + 1) * P],
                                                                table[:, ds(k + b, 1), q, :].rearrange("p b c -> p (b c)"),
                                                                start=False, stop=False)
                            last.then_inc(s_exp1, 1)
                            pe.reg_add(wn1_pe, wn1_pe, 1)
                        nc.tensor.matmul(psum_exp[j % 2][:, 0:G * CT], zeros[0:1, 0:P], zeros[0:1, 0:G * CT], start=False, stop=True)
                        pe.wait_ge(s_msg, g + 2)
                        pe.sem_inc(s_seen, 1)
                        pe.wait_ge(s_silu, g + 1)
                        for u in range(G):
                            last = nc.tensor.matmul(psum_gate[:, u * C:(u + 1) * C], hid[:, j % 2, u * P:(u + 1) * P], w2s[:, :],
                                                    start=True, stop=True)
                        last.then_inc(s_mlp, 1)
                        if j > 0 or not peeled:
                            combine(g - 1, (j - 1) % 2)

                turn(0, True)
                with pe.Fori(1, TURNS) as i:
                    turn(i, False)
                combine(NG - 1, (NG - 1) % 2)

            @block.scalar
            def _(act):
                act.sem_inc(s_out, 2)

                def part0(g, par):
                    act.wait_ge(s_msg, g + 3)
                    act.sem_inc(s_seen, 1)
                    nc.scalar.copy(parts[:, par, :, 0, :], prod[:, par, :, :]).then_inc(s_p0, 1)

                def part1(g, par):
                    act.wait_ge(s_r, g + 1)
                    act.sem_inc(s_seen, 1)
                    nc.scalar.copy(parts[:, par, :, 1, :], rest[:, :, :]).then_inc(s_p1, 1)

                def hand_over(g, slot):
                    act.wait_ge(s_comb, g + 1)
                    act.sem_inc(s_seen, 1)
                    act.wait_ge(s_landed, g + (GB - 1))
                    nc.scalar.activation(rows[:, slot * G:(slot + 1) * G, 0:CS],
                                         psum_comb[slot % 2][:, 0:G * CS].rearrange("p (g c) -> p g c", c=CS), ACT.Copy).then_inc(s_out, 1)

                def turn(i, peeled):
                    for j in range(GB):
                        g = i * GB + j
                        act.wait_ge(s_hid, g + 1)
                        nc.scalar.activation(hid[0:C, j % 2, :], psum_hid[0:C, :], ACT.Silu, bias=b1s[:, 0:1]).then_inc(s_silu, 1)
                        if j > 0 or not peeled:
                            part1(g - 1, (j - 1) % 2)
                        part0(g, j % 2)
                        if j > 0 or not peeled:
                            hand_over(g - 1, (j - 1) % GB)

                turn(0, True)
                with act.Fori(1, TURNS) as i:
                    turn(i, False)
                part1(NG - 1, (NG - 1) % 2)
                hand_over(NG - 1, GB - 1)

            @block.gpsimd
            def _(pool):
                pool.sem_inc(s_landed, GB)

                def turn(i, peeled):
                    for j in range(GB):
                        g = i * GB + j
                        pool.wait_ge(s_idx1, g + 1)
                        pool.sem_inc(s_seen, 1)
                        pool.wait_ge(s_out, g + 3)
                        pool.sem_inc(s_seen, 1)
                        for u in range(j * G, (j + 1) * G):
                            c = u % K
                            if u >= K or not peeled:
                                pool.wait_ge(s_scat[c], i * (16 * U // K) + 16 * (u // K))
                                pool.sem_inc(s_seen, 1)
                            pool.indirect_dma_start(out=sums[c], out_offset=bass.IndirectOffsetOnAxis(ap=idx[:, u:u + 1], axis=0),
                                                    in_=rows[:, u, 0:CS], in_offset=None, compute_op=ALU.add).then_inc(s_scat[c], 16)
                        pool.sem_inc(s_landed, 1)

                turn(0, True)
                with pool.Fori(1, TURNS) as i:
                    turn(i, False)
                for c in range(K):
                    pool.wait_ge(s_scat[c], 16 * T // K)

        s_var2 = sem("s_var2"); s_std2 = sem("s_std2"); s_exped = sem("s_exped")
        s_sum = [sem(f"s_sum{r}") for r in range(3)]
        s_used = sem("s_used"); s_t2 = sem("s_t2"); s_t2out = sem("s_t2out")
        n49 = NB * CS
        copies = [tbl_flat[:, 0:n49], scratch[:, 0:n49]]
        flat_acc = acc_flat[:, 0:n49]
        t2 = tbl_flat[:, 0:n49].rearrange("p (b c) -> p b c", c=CS)
        with nc.Block() as block:
            @block.sync
            def _(sp):
                sp.dma_start(flat_acc, sums[0][0:NPAD, :].rearrange("(p b) c -> p (b c)", p=P)).then_inc(s_sum[2], 16)
                for c in range(1, K):
                    if c >= 3:
                        sp.wait_ge(s_used, c - 2)
                    sp.dma_start(copies[c % 2], sums[c][0:NPAD, :].rearrange("(p b) c -> p (b c)", p=P)).then_inc(s_sum[c % 2], 16)
                sp.wait_ge(s_t2, 1)
                sp.dma_start(table2.rearrange("(p b) c -> p (b c)", p=P), tbl_flat[:, 0:n49]).then_inc(s_t2out, 16)
                sp.wait_ge(s_t2out, 16)

            @block.vector
            def _(dve):
                link = chain(dve, "s_epi1_chain")
                dve.wait_ge(s_sum[2], 16)
                for c in range(1, K):
                    dve.wait_ge(s_sum[c % 2], 16 * ((c + 1) // 2))
                    nv.tensor_tensor(flat_acc, flat_acc, copies[c % 2], ALU.add).then_inc(s_used, 1)
                    dve.wait_ge(s_used, c)
                tot = stat[:, 0, :]
                link(nv.tensor_scalar(tot, acc[:, 0:NB, C], 1e-8, None, ALU.max))
                link(nv.reciprocal(stat[:, 1, :], tot))
                link(nv.tensor_tensor(acc[:, 0:NB, 0:C], acc[:, 0:NB, 0:C], stat[:, 1, :].unsqueeze(2).to_broadcast([P, NB, C]), ALU.mult))
                link(nv.tensor_tensor(h[:, :, :], h[:, :, :], acc[:, 0:NB, 0:C], ALU.add))
                layernorm_relu(link, nv, None, s_var2, s_std2, 0, h[:, :, :], acc[:, 0:NB, 0:C], gammab[:, :], betab[:, :])
                link(nv.tensor_tensor(nodes[:, :, :], nodes[:, :, :], acc[:, 0:NB, 0:C], ALU.add))
                layernorm_relu(link, nv, None, s_var2, s_std2, 1, nodes[:, :, :], h[:, :, :])
                link(nv.memset(t2[:, :, C:CS], 1.0))
                nv.tensor_copy(t2[:, :, 0:C], h[:, :, :]).then_inc(s_t2, 1)

            @block.scalar
            def _(act):
                std(act, s_var2, s_std2, 0)
                std(act, s_var2, s_std2, 1)
                nc.scalar.activation(lg[:, :], lg[:, :], ACT.Exp).then_inc(s_exped, 1)

        spmm_pass(1, "l2", table2, CS, lg, False)

        def table_out(sp, s_made, s_landed, dram_table, src):
            sp.wait_ge(s_made, 1)
            sp.dma_start(dram_table.rearrange("(p b) c -> p (b c)", p=P), src).then_inc(s_landed, 16)
            sp.wait_ge(s_landed, 16)

        s_var3 = sem("s_var3"); s_std3 = sem("s_std3"); s_neg = sem("s_neg"); s_elu = sem("s_elu")
        s_h3 = sem("s_h3"); s_h3out = sem("s_h3out")
        e3 = scratch[:, 0:NB * C].rearrange("p (b c) -> p b c", c=C)
        with nc.Block() as block:
            @block.sync
            def _(sp):
                table_out(sp, s_h3, s_h3out, table3[0], h_flat)

            @block.vector
            def _(dve):
                link = chain(dve, "s_epi2_chain")
                a3 = acc[:, 0:NB, 0:C]
                link(nv.tensor_scalar(stat[:, 0, :], acc[:, 0:NB, C], 1e-30, None, ALU.max))
                link(nv.reciprocal(stat[:, 1, :], stat[:, 0, :]))
                link(nv.tensor_tensor(a3, a3, stat[:, 1, :].unsqueeze(2).to_broadcast([P, NB, C]), ALU.mult))
                nv.tensor_scalar(e3, a3, 0.0, None, ALU.min).then_inc(s_neg, 1)
                link(nv.tensor_scalar(a3, a3, 0.0, -1.0, ALU.max, ALU.add))
                link(nv.tensor_tensor(nodes[:, :, :], nodes[:, :, :], a3, ALU.add))
                dve.wait_ge(s_elu, 1)
                link(nv.tensor_tensor(nodes[:, :, :], nodes[:, :, :], e3, ALU.add))
                layernorm_relu(link, nv, None, s_var3, s_std3, 0, nodes[:, :, :], h[:, :, :])
                nv.memset(stat[:, 0, 0:1], 0.0).then_inc(s_h3, 1)

            @block.scalar
            def _(act):
                act.wait_ge(s_neg, 1)
                nc.scalar.activation(scratch[:, 0:NB * C], scratch[:, 0:NB * C], ACT.Exp).then_inc(s_elu, 1)
                std(act, s_var3, s_std3, 0)

        spmm_pass(2, "l3a", table3[0], C, w, False)
        s_y1 = sem("s_y1"); s_y1out = sem("s_y1out")
        third = 1.0 / (LAYERS + 1)
        with nc.Block() as block:
            @block.sync
            def _(sp):
                table_out(sp, s_y1, s_y1out, table3[1], scratch[:, 0:NB * C])

            @block.vector
            def _(dve):
                link = chain(dve, "s_epi3_chain")
                nv.tensor_copy(e3, acc[:, 0:NB, 0:C]).then_inc(s_y1, 1)
                link(nv.tensor_tensor(h[:, :, :], h[:, :, :], acc[:, 0:NB, 0:C], ALU.add))
                link(nv.scalar_tensor_tensor(out=nodes[:, :, :], in0=h[:, :, :], scalar=third, in1=nodes[:, :, :], op0=ALU.mult, op1=ALU.add))

        spmm_pass(3, "l3b", table3[1], C, w, False)
        s_res = sem("s_res"); s_resout = sem("s_resout")
        with nc.Block() as block:
            @block.vector
            def _(dve):
                nv.scalar_tensor_tensor(out=nodes[:, :, :], in0=acc[:, 0:NB, 0:C], scalar=third, in1=nodes[:, :, :],
                                        op0=ALU.mult, op1=ALU.add).then_inc(s_res, 1)

            @block.sync
            def _(sp):
                sp.wait_ge(s_res, 1)
                sp.dma_start(out, nodes[:, :, :].rearrange("p b c -> p (b c)")).then_inc(s_resout, 16)
                sp.wait_ge(s_resout, 16)


def kernel(x, src, dst, edge_attr_40, edge_weight, edge_weight1, node_type_119, node_vec, L1_gnn_W1, L1_gnn_b1,
           L1_gnn_W2, L1_gnn_b2, L1_gnn_emb, L1_gnn_adaptW, L1_gnn_gamma, L1_gnn_beta):
    import numpy as np
    import concourse.bacc as bacc
    from concourse.bass_utils import run_bass_kernel_spmd

    def padded(a, n, fill=0):
        a = np.asarray(a)
        return np.concatenate([a, np.full((n - a.shape[0],) + a.shape[1:], fill, a.dtype)])

    def node_major(a):
        a = padded(a, NPAD)
        a = a.reshape(NB, P, -1).transpose(1, 0, 2)
        return a.reshape(P, -1)

    ne = T * P
    last = NPAD - 1
    s, d = padded(src, ne, last), padded(dst, ne, last)
    ew, lgt = padded(edge_weight, ne), padded(np.asarray(edge_weight1)[:, 0], ne)
    arrays = {
        "x": node_major(x),
        "dst_cols": d.reshape(T, P).T, "src_cols": s.reshape(T, P).T,
        "dst_rows": d.reshape(NG, GW), "src_rows": s.reshape(NG, GW),
        "w_cols": ew.reshape(T, P).T, "logit_cols": lgt.reshape(T, P).T, "logit_rows": lgt.reshape(NG, GW),
        "attr_t": padded(edge_attr_40, ne).T,
        "type_row": padded(node_type_119, NPAD).reshape(1, NPAD),
        "mult": node_major(node_vec),
        "w1_t": np.asarray(L1_gnn_W1).T, "b1": np.asarray(L1_gnn_b1).reshape(C, 1),
        "w2e": np.concatenate([np.asarray(L1_gnn_W2).T, np.asarray(L1_gnn_b2).reshape(1, C)]),
        "emb": np.asarray(L1_gnn_emb), "emb_t": np.asarray(L1_gnn_emb).T, "adapt_t": np.asarray(L1_gnn_adaptW).T,
        "gamma": np.asarray(L1_gnn_gamma), "beta": np.asarray(L1_gnn_beta),
    }
    arrays = {f"in_{k}": np.ascontiguousarray(v) for k, v in arrays.items()}
    nc = bacc.Bacc("TRN2", target_bir_lowering=False, num_devices=1)
    args = [nc.dram_tensor(k, v.shape, mybir.dt.from_np(v.dtype), kind="ExternalInput").ap() for k, v in arrays.items()]
    out = nc.dram_tensor("out", (P, NB * C), mybir.dt.float32, kind="ExternalOutput").ap()
    gnn_kernel(nc, *args, out)
    r = run_bass_kernel_spmd(nc, [arrays], core_ids=[0])
    y = np.asarray(r.results[0]["out"]).reshape(P, NB, C).transpose(1, 0, 2).reshape(NPAD, C)
    return np.ascontiguousarray(y[:N])
```

```python
import concourse.bass as bass
from concourse import mybir
from contextlib import ExitStack

N = 12500
C = 48
E = 212500
R = 40
NEL = 119
GE = 32
P = 128
NB_BITS = 7
NB = -(-N // P)
NPAD = NB * P
NBW = NB + 2
G = 4
RING = 4
GB = 2 * RING
U = G * GB
NG = -(-E // (P * U)) * GB
T = NG * G
TURNS = NG // GB
GS = 4
QS = NG // GS
GW = G * P
AHEAD = 3
TI = T + AHEAD * G
PARTS = 3
C0 = C + GE
CS = C + 1
CT = C + 2
K = 8
TRASH = NPAD
NR = NPAD + P
CLEARS = 24
CLEARED = NR // CLEARS
CLEARED_P = 66
CUTOFF = 6.0
LN_EPS = 1e-5
BIG = 2.0 ** 100
LAYERS = 2
ZB = 7
ZR = 3
PI = 3.141592653589793


def gnn_kernel(nc, x, dst_cols, src_cols, dst_rows, src_rows, w_cols, logit_cols, logit_rows,
               attr_t, type_row, mult, w1_t, b1, w2e, emb, emb_t, adapt_t, gamma, beta, out):
    f32 = mybir.dt.float32
    i32 = mybir.dt.int32
    u16 = mybir.dt.uint16
    bf16 = mybir.dt.bfloat16
    ALU = mybir.AluOpType
    ACT = mybir.ActivationFunctionType
    X_AXIS = mybir.AxisListType.X
    ds = bass.ds

    with ExitStack() as ctx:
        def sb(name, shape, dt=f32):
            return ctx.enter_context(nc.sbuf_tensor(name, shape, dt))

        def sem(name):
            return ctx.enter_context(nc.semaphore(name))

        def dram(name, shape, dt=f32):
            return nc.dram_tensor(name, shape, dt, kind="Internal").ap()

        table0 = dram("table0", (NPAD, C0))
        table2 = dram("table2", (NPAD, CS))
        table3 = [dram(f"table3_{k}", (NPAD, C)) for k in range(LAYERS)]
        sums = [dram(f"sums{k}", (NR, CS)) for k in range(K)]
        rows16_dram = dram("rows16_dram", (2, NG, GW), u16)
        hid_dram = dram("hid_dram", (C, NG * GW))
        ranges_dram = dram("ranges_dram", (QS, GS * 2), i32)

        nodes = sb("nodes", [P, NB, C])
        h = sb("h", [P, NB, C])
        acc = sb("acc", [P, NBW, CS])
        table = sb("table", [P, NBW, PARTS, CT], bf16)
        embq = table[:, :, :, :].rearrange("p b k c -> p (b k c)")[:, 0:NBW * PARTS * GE].rearrange("p (b k c) -> p b k c", k=PARTS, c=GE)
        scratch = sb("scratch", [P, NB * CS + 16])
        iota = sb("iota", [P, NBW * P], u16)
        dstf = sb("dstf", [P, TI])
        w = sb("w", [P, TI])
        cw = sb("cw", [P, T])
        lg = sb("lg", [P, TI])
        adapt = sb("adapt", [P, G + T])
        srow = sb("srow", [P, TI])
        ranges = sb("ranges", [1, NG * 2], i32)
        node = sb("node", [P, NBW])
        segmax = sb("segmax", [P, NBW])
        multc = sb("multc", [P, NB])
        gammab = sb("gammab", [P, C])
        betab = sb("betab", [P, C])
        w1s = sb("w1s", [R, C])
        b1s = sb("b1s", [C, 1])
        w2s = sb("w2s", [C + 1, C])
        lower = sb("lower", [P, P], bf16)
        trash = sb("trash", [P, 1])
        zeros = sb("zeros", [1, G * CT], bf16)
        idx = sb("idx", [P, RING * G], i32)
        rows = sb("rows", [P, RING * G, C0])
        onehot = sb("onehot", [P, G, P], bf16)
        onet = sb("onet", [P, GW], bf16)
        same = sb("same", [P, 2, G, P], bf16)
        drow = sb("drow", [P, 2, GW], u16)
        srcrow = sb("srcrow", [P, 2, GW], u16)
        lrow = sb("lrow", [P, 2, GW])
        attr = [srcrow[0:R, :, :].rearrange("p r e -> p (r e)").bitcast(f32), same[0:R, :, :, :].rearrange("p r u e -> p (r u e)").bitcast(f32)]
        hid = sb("hid", [C + 1, 2, GW])
        gate = sb("gate", [P, 2, G, CS])
        prod = sb("prod", [P, 2, G, CS])
        rest = sb("rest", [P, G, CS])
        parts = sb("parts", [P, 2, G, PARTS, CS], bf16)
        dup = sb("dup", [P, G])
        dmp = sb("dmp", [P, G])
        wmax = sb("wmax", [P, 1])
        warm = sb("warm", [C, 1])
        far = sb("far", [P, NBW])
        dots = sb("dots", [P, G, GE])
        adaptg = sb("adaptg", [P, G])
        pen = scratch[:, 0:GW]
        junk = scratch[:, GW:2 * GW]
        def ps(name, shape):
            return ctx.enter_context(nc.psum_tensor(name, shape, f32))

        psum_acc = ps("psum_acc", [P, 512])
        psum_exp = [ps(f"psum_exp{r}", [P, 512]) for r in range(2)]
        psum_mlp = [ps(f"psum_mlp{r}", [P, 512]) for r in range(2)]
        psum_comb = [ps(f"psum_comb{r}", [P, 512]) for r in range(2)]

        zc = scratch[0:NEL, 0:ZR * ZB * P].bitcast(i32).rearrange("p (r n) -> p r n", r=ZR)
        zhot = scratch[0:NEL, ZR * ZB * P:(ZR + 2) * ZB * P].rearrange("p (r n) -> p r n", r=2)
        typec = sb("typec", [P, 1])
        ea = sb("ea", [NEL, 2 * GE])
        embts = sb("embts", [GE, NEL])
        adapts = sb("adapts", [GE, GE])
        stat = sb("stat", [P, 4, NB])
        tbl_flat = table[:, :, :, :].rearrange("p b k c -> p (b k c)").bitcast(f32)
        acc_flat = acc[:, :, :].rearrange("p b c -> p (b c)")
        h_flat = h[:, :, :].rearrange("p b c -> p (b c)")
        int_a = tbl_flat[:, 0:T].bitcast(i32)
        int_b = tbl_flat[:, T:2 * T].bitcast(i32)
        int_c = tbl_flat[:, 2 * T:3 * T].bitcast(i32)
        embst = tbl_flat[:, -NB * GE:].rearrange("p (b c) -> p b c", c=GE)
        embq32 = acc_flat[:, 0:NB * GE].rearrange("p (b c) -> p b c", c=GE)
        clear = scratch[0:CLEARED_P, -(CLEARED // CLEARED_P * CS):]
        dr_i = h_flat[0:QS, 0:GS * GW].bitcast(i32)
        sr_i = h_flat[0:QS, GS * GW:2 * GS * GW].bitcast(i32)
        rows16 = scratch[0:QS, GS * GW:2 * GS * GW].bitcast(u16).rearrange("q (k e) -> q k e", k=2)
        wk_i = stat[:, :, :].rearrange("p a b -> p (a b)").bitcast(i32)

        def by_partition(t, c):
            return t.rearrange("(p b) c -> p b c", p=P)[:, :, c[0]:c[1]]

        def layernorm_relu(link, nv, s_var, s_std, turn, src, dst, mul=None, room=None, made=None):
            squares = scratch[:, 0:NB * C].rearrange("p (b c) -> p b c", c=C) if room is None else room
            step = NB if room is None else NB // 2
            s, v, r = stat[:, 0, :], stat[:, 1, :], stat[:, 2, :]
            bc = lambda a: a.unsqueeze(2).to_broadcast([P, NB, C])
            link(nv.tensor_reduce(out=s, in_=src, axis=X_AXIS, op=ALU.add))
            link(nv.tensor_scalar(s, s, 1.0 / C, None, ALU.mult))
            link(nv.tensor_tensor(dst, src, bc(s), ALU.subtract))
            for b in range(0, NB, step):
                link(nv.tensor_tensor(squares, dst[:, b:b + step, :], dst[:, b:b + step, :], ALU.mult))
                link(nv.tensor_reduce(out=v[:, b:b + step], in_=squares, axis=X_AXIS, op=ALU.add))
            nv.tensor_scalar(v, v, 1.0 / C, LN_EPS, ALU.mult, ALU.add).then_inc(s_var, 1)
            nv.wait_ge(s_std, turn + 1)
            link(nv.reciprocal(r, stat[:, 3, :]))
            if mul is None:
                for b in range(0, NB, NB // 2):
                    half = dst[:, b:b + NB // 2, :]
                    last = nv.scalar_tensor_tensor(out=half, in0=half, scalar=0.0,
                                                   in1=r[:, b:b + NB // 2].unsqueeze(2).to_broadcast([P, NB // 2, C]),
                                                   op0=ALU.max, op1=ALU.mult)
                    if made is None:
                        link(last)
                    else:
                        last.then_inc(made, 1)
            else:
                link(nv.tensor_tensor(dst, dst, bc(r), ALU.mult))
                link(nv.tensor_tensor(dst, dst, mul.unsqueeze(1).to_broadcast([P, NB, C]), ALU.mult))

        def split(link, to, x, left):
            link(nv.tensor_copy(to[:, :, 0, :], x))
            link(nv.tensor_tensor(left, x, to[:, :, 0, :], ALU.subtract))
            link(nv.tensor_copy(to[:, :, 1, :], left))
            link(nv.tensor_tensor(to[:, :, 2, :], left, to[:, :, 1, :], ALU.subtract))

        def std(act, s_var, s_std, turn):
            act.wait_ge(s_var, turn + 1)
            nc.scalar.activation(stat[:, 3, :], stat[:, 1, :], ACT.Sqrt).then_inc(s_std, 1)

        def chain(eng, name):
            s, n = sem(name), [0]

            def link(instruction):
                n[0] += 1
                instruction.then_inc(s, 1)
                eng.wait_ge(s, n[0])
            return link

        def table_out(sp, s_made, s_landed, dram_table, src):
            half = src.shape[1] // 2
            for k in range(2):
                sp.wait_ge(s_made, k + 1)
                sp.dma_start(dram_table.rearrange("(p b) c -> p (b c)", p=P)[:, k * half:(k + 1) * half],
                             src[:, k * half:(k + 1) * half]).then_inc(s_landed, 16)
            sp.wait_ge(s_landed, 32)

        nv = nc.vector

        s_x = sem("s_x"); s_ints = sem("s_ints"); s_rowints = sem("s_rowints"); s_w = sem("s_w")
        s_lg = sem("s_lg"); s_small = sem("s_small"); s_consts = sem("s_consts")
        s_srowd = sem("s_srowd"); s_srowout = sem("s_srowout"); s_ranged = sem("s_ranged")
        s_rangeout = sem("s_rangeout"); s_rangein = sem("s_rangein")
        s_zin = [sem(f"s_zin{r}") for r in range(ZR)]
        s_zhot = sem("s_zhot"); s_zmm = sem("s_zmm"); s_zout = sem("s_zout")
        s_ea = sem("s_ea"); s_eamm = sem("s_eamm")
        s_var = sem("s_var"); s_std = sem("s_std")
        s_h0 = sem("s_h0"); s_table0 = sem("s_table0"); s_sin = sem("s_sin"); s_sinin = sem("s_sinin")
        s_typec = sem("s_typec"); s_embout = sem("s_embout")
        ZT = NB // ZB
        with nc.Block() as block:
            @block.sync
            def _(sp):
                sp.dma_start(int_a, src_cols).then_inc(s_ints, 16)
                sp.dma_start(int_b, dst_cols).then_inc(s_ints, 16)
                sp.dma_start(dr_i, dst_rows.rearrange("(q j) e -> q (j e)", j=GS)).then_inc(s_rowints, 16)
                sp.dma_start(sr_i, src_rows.rearrange("(q j) e -> q (j e)", j=GS)).then_inc(s_rowints, 16)
                sp.dma_start(w[:, 0:T], w_cols).then_inc(s_w, 16)
                sp.dma_start(nodes[:, :, :].rearrange("p b c -> p (b c)"), x).then_inc(s_x, 16)
                sp.dma_start(lg[:, 0:T], logit_cols).then_inc(s_lg, 16)
                sp.wait_ge(s_srowd, 1)
                for k in range(2):
                    sp.dma_start(rows16_dram[k].rearrange("(q j) e -> q (j e)", j=GS), rows16[:, k, :]).then_inc(s_srowout, 16)
                sp.wait_ge(s_ranged, 1)
                sp.dma_start(ranges_dram, idx[0:QS, 0:2 * GS]).then_inc(s_rangeout, 16)
                sp.wait_ge(s_rangeout, 16)
                sp.dma_start(ranges[0:1, :], ranges_dram.rearrange("q j -> (q j)").unsqueeze(0)).then_inc(s_rangein, 16)
                sp.wait_ge(s_rangein, 16)
                sp.wait_ge(s_srowout, 32)
                sp.wait_ge(s_lg, 16)

            @block.gpsimd
            def _(pool):
                nc.gpsimd.iota(iota[:, :], pattern=[[1, NBW * P]], base=0, channel_multiplier=0).then_inc(s_consts, 1)
                nc.gpsimd.memset(lower[:, :], 1.0).then_inc(s_consts, 1)
                pool.wait_ge(s_consts, 2)
                nc.gpsimd.affine_select(out=lower[:, :], in_=lower[:, :], compare_op=ALU.is_gt, fill=0.0,
                                        base=0, pattern=[[-1, P]], channel_multiplier=1).then_inc(s_consts, 1)

            @block.scalar
            def _(act):
                act.dma_start(multc[:, :], mult).then_inc(s_small, 16)
                act.dma_start(gammab[:, :], gamma.partition_broadcast(P)).then_inc(s_small, 16)
                act.dma_start(betab[:, :], beta.partition_broadcast(P)).then_inc(s_small, 16)
                act.dma_start(w1s[:, :], w1_t).then_inc(s_small, 16)
                act.dma_start(b1s[:, :], b1).then_inc(s_small, 16)
                act.dma_start(w2s[:, :], w2e).then_inc(s_small, 16)
                act.dma_start(ea[:, 0:GE], emb).then_inc(s_small, 16)
                act.dma_start(embts[:, :], emb_t).then_inc(s_small, 16)
                act.dma_start(adapts[:, :], adapt_t).then_inc(s_small, 16)
                act.wait_ge(s_small, 9 * 16)

            @block.vector
            def _(dve):
                link = chain(dve, "s_setup_chain")
                nv.memset(zeros[:, :], 0.0)
                nv.memset(segmax[:, :], -BIG)
                for columns in (srow, dstf, w, lg):
                    nv.memset(columns[:, T:TI], 0.0)
                nv.memset(hid[:, :, :], 1.0)
                nv.memset(gate[:, :, :, :], 1.0)
                nv.memset(adaptg[:, :], 0.0)
                dve.wait_ge(s_ints, 32)
                nv.tensor_copy(dstf[:, 0:T], int_b)
                link(nv.tensor_scalar(int_c, int_a, NB_BITS, None, ALU.logical_shift_right))
                link(nv.tensor_scalar(int_a, int_a, P - 1, None, ALU.bitwise_and))
                link(nv.scalar_tensor_tensor(out=srow[:, 0:T], in0=int_a, scalar=float(NB), in1=int_c, op0=ALU.mult, op1=ALU.add))
                dve.wait_ge(s_rowints, 32)
                tmp = scratch[0:QS, 0:GS * GW].bitcast(i32)
                link(nv.tensor_scalar(tmp, sr_i, NB_BITS, None, ALU.logical_shift_right))
                link(nv.tensor_scalar(sr_i, sr_i, P - 1, None, ALU.bitwise_and))
                nv.tensor_copy(rows16[:, 0, :], dr_i)
                nv.scalar_tensor_tensor(out=rows16[:, 1, :], in0=sr_i, scalar=float(NB),
                                        in1=tmp, op0=ALU.mult, op1=ALU.add).then_inc(s_srowd, 1)
                d4 = dr_i.rearrange("q (j e) -> q j e", j=GS)
                lo = wk_i[0:QS, 0:GS]
                hi = wk_i[0:QS, GS:2 * GS]
                link(nv.tensor_reduce(out=lo, in_=d4, axis=X_AXIS, op=ALU.min))
                link(nv.tensor_reduce(out=hi, in_=d4, axis=X_AXIS, op=ALU.max))
                link(nv.tensor_scalar(lo, lo, NB_BITS, None, ALU.logical_shift_right))
                link(nv.tensor_scalar(hi, hi, NB_BITS, None, ALU.logical_shift_right))
                pairs = idx[0:QS, 0:2 * GS].rearrange("q (j k) -> q j k", k=2)
                link(nv.tensor_copy(pairs[:, :, 0], lo))
                link(nv.tensor_scalar(pairs[:, :, 1], hi, 1.0, None, ALU.add))
                nv.memset(stat[:, 3, 1:2], 0.0).then_inc(s_ranged, 1)

        with nc.Block() as block:
            @block.sync
            def _(sp):
                sp.wait_ge(s_zout, ZT)
                sp.dma_start(by_partition(table0, (C, C0)), embst).then_inc(s_embout, 16)
                for k in range(2):
                    sp.wait_ge(s_h0, k + 1)
                    sp.dma_start(by_partition(table0, (0, C))[:, k * NB // 2:(k + 1) * NB // 2, :],
                                 h[:, k * NB // 2:(k + 1) * NB // 2, :]).then_inc(s_table0, 16)
                sp.wait_ge(s_table0, 32)
                sp.wait_ge(s_embout, 16)

            @block.gpsimd
            def _(pool):
                nc.gpsimd.iota(int_a[:, 0:1], pattern=[[0, 1]], base=0, channel_multiplier=1).then_inc(s_consts, 1)
                nc.gpsimd.iota(int_a[:, 1:1 + NBW], pattern=[[P, NBW]], base=0, channel_multiplier=1).then_inc(s_consts, 1)
                nc.gpsimd.iota(int_a[:, 1 + NBW:2 + NBW], pattern=[[0, 1]], base=TRASH, channel_multiplier=1).then_inc(s_consts, 1)
                pool.wait_ge(s_typec, 1)
                for q in range(ZT):
                    pool.wait_ge(s_zin[q % ZR], 16 * (q // ZR + 1))
                    if q >= 2:
                        pool.wait_ge(s_zmm, q - 1)
                    nc.gpsimd.tensor_scalar(zhot[:, q % 2, :], zc[:, q % ZR, :], typec[0:NEL, 0:1], None,
                                            ALU.is_equal).then_inc(s_zhot, 1)

            @block.vector
            def _(dve):
                link = chain(dve, "s_const_chain")
                dve.wait_ge(s_consts, 6)
                nv.tensor_copy(typec[:, :], int_a[:, 0:1]).then_inc(s_typec, 1)
                dve.wait_ge(s_eamm, 1)
                link(nv.tensor_copy(node[:, :], int_a[:, 1:1 + NBW]))
                link(nv.tensor_copy(trash[:, :], int_a[:, 1 + NBW:2 + NBW]))
                link(nv.tensor_scalar(far[:, :], node[:, :], -BIG, None, ALU.mult))
                nv.tensor_copy(ea[:, GE:2 * GE], psum_mlp[0][0:NEL, 0:GE]).then_inc(s_ea, 1)
                room = tbl_flat[:, 0:NB // 2 * C].rearrange("p (b c) -> p b c", c=C)
                layernorm_relu(link, nv, s_var, s_std, 0, nodes[:, :, :], h[:, :, :], room=room, made=s_h0)
                a, b = int_a.bitcast(f32), int_b
                k12 = 2 * CUTOFF
                link(nv.tensor_scalar(a, w[:, 0:T], -1.0, None, ALU.mult))
                link(nv.tensor_tensor(a, a, w[:, 0:T], ALU.max))
                link(nv.tensor_scalar(b, a, 1.0 / k12, None, ALU.mult))
                link(nv.scalar_tensor_tensor(out=a, in0=b, scalar=-k12, in1=a, op0=ALU.mult, op1=ALU.add))
                c = cw[:, :]
                link(nv.tensor_scalar(c, a, -1.0, None, ALU.mult))
                link(nv.tensor_tensor(a, a, c, ALU.max))
                link(nv.tensor_scalar(c, a, -1.0, k12, ALU.mult, ALU.add))
                link(nv.tensor_tensor(a, a, c, ALU.min))
                nv.tensor_scalar(a, a, -PI / CUTOFF, PI / 2, ALU.mult, ALU.add).then_inc(s_sinin, 1)
                dve.wait_ge(s_sin, 1)
                link(nv.tensor_scalar(c, c, 0.5, 0.5, ALU.mult, ALU.add))
                link(nv.scalar_tensor_tensor(out=c, in0=w[:, 0:T], scalar=CUTOFF, in1=c, op0=ALU.is_lt, op1=ALU.mult))
                dve.wait_ge(s_zout, ZT)
                dve.wait_ge(s_embout, 16)
                link(nv.memset(embq[:, NB:NBW, :, :], 0.0))
                split(link, embq[:, 0:NB, :, :], embq32, scratch[:, 0:NB * GE].rearrange("p (b c) -> p b c", c=GE))

            @block.tensor
            def _(pe):
                nc.tensor.matmul(psum_mlp[0][0:NEL, 0:GE], embts[:, :], adapts[:, :], start=True, stop=True).then_inc(s_eamm, 1)
                pe.wait_ge(s_ea, 1)
                for q in range(ZT):
                    pe.wait_ge(s_zhot, q + 1)
                    if q >= 2:
                        pe.wait_ge(s_zout, q - 1)
                    for b in range(ZB):
                        last = nc.tensor.matmul(psum_exp[q % 2][:, b * 2 * GE:(b + 1) * 2 * GE],
                                                zhot[:, q % 2, b * P:(b + 1) * P], ea[:, :], start=True, stop=True)
                    last.then_inc(s_zmm, 1)

            @block.scalar
            def _(act):
                for q in range(min(ZR, ZT)):
                    act.dma_start(zc[:, q, :], type_row[0, q * ZB * P:(q + 1) * ZB * P].partition_broadcast(NEL)).then_inc(s_zin[q], 16)
                for q in range(ZT):
                    if q == ZT - 2:
                        act.wait_ge(s_sinin, 1)
                        nc.scalar.activation(cw[:, :], int_a.bitcast(f32), ACT.Sin).then_inc(s_sin, 1)
                    act.wait_ge(s_zmm, q + 1)
                    pv = psum_exp[q % 2][:, 0:ZB * 2 * GE].rearrange("p (b c) -> p b c", c=2 * GE)
                    nc.scalar.copy(embst[:, q * ZB:(q + 1) * ZB, :], pv[:, :, 0:GE])
                    nc.scalar.copy(embq32[:, q * ZB:(q + 1) * ZB, :], pv[:, :, GE:2 * GE]).then_inc(s_zout, 1)
                    if q == 5:
                        std(act, s_var, s_std, 0)
                    if q + ZR < ZT:
                        act.dma_start(zc[:, q % ZR, :], type_row[0, (q + ZR) * ZB * P:(q + ZR + 1) * ZB * P].partition_broadcast(NEL)).then_inc(s_zin[q % ZR], 16)

        s_rows = [sem(f"s_rows{j}") for j in range(RING)]
        s_prod32 = sem("s_prod32")
        s_part0 = sem("s_part0")
        s_rest = sem("s_rest")
        s_part1 = sem("s_part1")
        s_part2 = sem("s_part2")
        s_hot = sem("s_hot")
        s_mm = sem("s_mm")
        s_added = sem("s_added")
        s_onet = sem("s_onet")
        s_exp = sem("s_exp")
        s_pen = sem("s_pen")
        s_wmax = sem("s_wmax")
        s_maxed = sem("s_maxed")
        s_closed = sem("s_closed")
        s_seen = sem("s_seen")
        wn_dve = nc.vector.alloc_register("dve_window")
        wn_act = nc.scalar.alloc_register("act_window")
        wn_pe = nc.tensor.alloc_register("pe_window")
        range_regs = {e: [e.alloc_register(f"range{k}_{n}") for k in range(2 * GB)]
                      for n, e in (("dve", nc.vector), ("pe", nc.tensor), ("act", nc.scalar))}

        def load_ranges(eng, i):
            regs = range_regs[eng]
            eng.load(regs, ranges[0:1, ds(i * (2 * GB), 2 * GB)])
            return [(eng.snap(regs[2 * j], min_val=0, max_val=NB - 1), eng.snap(regs[2 * j + 1], min_val=1, max_val=NB))
                    for j in range(GB)]

        def spmm_pass(order, name, src_table, cols, weights, first):
            s_idx = sem(name + "_idx")
            s_free = sem(name + "_free")
            s_clear = sem(name + "_clear")
            if first:
                s_zero = sem(name + "_zero")
                s_cleared = sem(name + "_cleared")
                s_bcast = [sem(f"{name}_bcast{r}") for r in range(2)]
                s_attr = [sem(f"{name}_attr{r}") for r in range(2)]
                s_mlp1 = sem(name + "_mlp1")
                s_hid = sem(name + "_hid")
                s_hidout = [sem(f"{name}_hidout{r}") for r in range(2)]
            width = src_table.shape[1]
            past = order * (NG + 1)
            passed = order * NG

            with nc.Block() as block:
                @block.gpsimd
                def _(pool):
                    def gather(g, j):
                        pool.wait_ge(s_idx, g + 1)
                        pool.sem_inc(s_seen, 1)
                        for u in range(j % RING * G, (j % RING + 1) * G):
                            pool.indirect_dma_start(
                                out=rows[:, u, 0:width], out_offset=None, in_=src_table,
                                in_offset=bass.IndirectOffsetOnAxis(ap=idx[:, u:u + 1], axis=0)).then_inc(s_rows[j % RING], 16)

                    with pool.Fori(0, TURNS) as i:
                        for j in range(GB):
                            gather(i * GB + j, j)
                    gather(NG, NG)

                if first:
                    @block.sync
                    def _(sp):
                        for r in range(2):
                            sp.sem_inc(s_hidout[r], 16)
                        sp.wait_ge(s_zero, 1)

                        def store_hidden(g, par):
                            sp.wait_ge(s_hid, g + 3)
                            sp.sem_inc(s_seen, 1)
                            sp.dma_start(hid_dram[:, ds(g * GW, GW)], hid[0:C, par, :]).then_inc(s_hidout[par], 16)

                        def load_pair(i, peeled):
                            for j in range(2):
                                sp.wait_ge(s_mlp1, i * 2 + (j + 1))
                                sp.sem_inc(s_seen, 1)
                                sp.dma_start(attr[j % 2], attr_t[:, ds((i * 2 + j) * GW, GW)]).then_inc(s_attr[j % 2], 16)
                                sp.wait_ge(s_free, i * 2 + (j + RING - 1))
                                sp.sem_inc(s_seen, 1)
                                sp.dma_start(drow[:, j % 2, :], rows16_dram[0, ds(i * 2 + j, 1), :].squeeze(0).partition_broadcast(P)).then_inc(s_bcast[j % 2], 16)
                                sp.dma_start(lrow[:, j % 2, :], logit_rows[ds(i * 2 + j, 1), :].squeeze(0).partition_broadcast(P)).then_inc(s_bcast[j % 2], 16)
                                if j >= 2 or not peeled:
                                    store_hidden(i * 2 + (j - 2), j % 2)

                        load_pair(0, True)
                        for c in range(K):
                            with sp.Fori(1 + c * CLEARS, 1 + (c + 1) * CLEARS) as i:
                                load_pair(i, False)
                                sp.dma_start(sums[c][ds((i - (1 + c * CLEARS)) * CLEARED, CLEARED), :].rearrange("(p r) c -> p (r c)", p=CLEARED_P),
                                             clear).then_inc(s_cleared, 16)
                        with sp.Fori(1 + K * CLEARS, NG // 2) as i:
                            load_pair(i, False)
                        for g in (NG - 2, NG - 1):
                            store_hidden(g, g % 2)
                        for r in range(2):
                            sp.wait_ge(s_hidout[r], 16 + 16 * NG // 2)
                        sp.wait_ge(s_cleared, K * CLEARS * 16)

                @block.scalar
                def _(act):
                    def stage(slot, column):
                        nc.scalar.copy(idx[:, slot * G:(slot + 1) * G], srow[:, ds(column, G)]).then_inc(s_idx, 1)

                    def part0(g, par):
                        act.wait_ge(s_prod32, g + (past + 1))
                        act.sem_inc(s_seen, 1)
                        nc.scalar.copy(parts[:, par, :, 0, 0:cols], prod[:, par, :, 0:cols]).then_inc(s_part0, 1)

                    def part1(g, par):
                        act.wait_ge(s_rest, g + (past + 1))
                        act.sem_inc(s_seen, 1)
                        nc.scalar.copy(parts[:, par, :, 1, 0:cols], rest[:, :, 0:cols]).then_inc(s_part1, 1)

                    def weigh(i, j):
                        act.wait_ge(s_rows[j % RING], i * (GB // RING * 16 * G) + (j // RING + order * (NG // RING + (j % RING == 0)) + 1) * 16 * G)
                        act.sem_inc(s_seen, 1)
                        for u in range(G):
                            last = nc.scalar.activation(prod[:, j % 2, u, 0:cols], rows[:, j % RING * G + u, 0:cols], ACT.Copy,
                                                        scale=weights[:, ds(i * U + (j * G + u), 1)])
                        last.then_inc(s_prod32, 1)

                    for j in range(AHEAD):
                        stage(j, j * G)
                    weigh(0, 0)
                    if first:
                        nc.scalar.activation(warm[:, :], b1s[:, :], ACT.Silu)
                        act.sem_inc(s_hid, 2)
                    part0(0, 0)
                    part1(0, 0)
                    if first:
                        act.reg_mov(wn_act, 1)
                    with act.Fori(0, TURNS) as i:
                        spans = load_ranges(act, i) if first else None
                        for j in range(GB):
                            if first:
                                act.wait_ge(s_bcast[j % 2], i * (16 * GB) + 32 * (j // 2 + 1))
                                act.sem_inc(s_seen, 1)
                                with act.Fori(*spans[j]) as k:
                                    win = act.snap(wn_act)
                                    act.wait_ge(s_maxed, win)
                                    act.sem_inc(s_seen, 1)
                                    nc.scalar.activation(pen[:, :], drow[:, j % 2, :], ACT.Abs, scale=BIG, bias=far[:, ds(k, 1)]).then_inc(s_pen, 1)
                                    act.reg_add(wn_act, wn_act, 1)
                                act.wait_ge(s_free, i * GB + (j + RING))
                                act.sem_inc(s_seen, 1)
                                nc.scalar.copy(adapt[:, ds(i * U + j * G, G)], adaptg[:, :])
                            stage((j + AHEAD) % RING, i * U + (j + AHEAD) * G)
                            weigh(i, j + 1)
                            part0(i * GB + (j + 1), (j + 1) % 2)
                            if first:
                                act.wait_ge(s_mlp1, i * GB + (j + 3))
                                act.sem_inc(s_seen, 1)
                                act.wait_ge(s_hidout[j % 2], i * (8 * GB) + 16 * (j // 2 + 1))
                                act.sem_inc(s_seen, 1)
                                nc.scalar.activation(hid[0:C, j % 2, :], psum_mlp[j % 2][0:C, :], ACT.Silu,
                                                     bias=b1s[:, 0:1]).then_inc(s_hid, 1)
                            part1(i * GB + (j + 1), (j + 1) % 2)
                    if first:
                        act.wait_ge(s_free, NG + RING)
                        nc.scalar.copy(adapt[:, T:T + G], adaptg[:, :])

                @block.vector
                def _(dve):
                    if first:
                        nv.memset(clear, 0.0).then_inc(s_zero, 1)
                    nv.memset(acc_flat, 0.0).then_inc(s_clear, 1)
                    dve.wait_ge(s_clear, 1)
                    if first:
                        dve.sem_inc(s_free, RING)
                        dve.sem_inc(s_added, 1)
                        dve.sem_inc(s_exp, 1)
                        dve.sem_inc(s_maxed, 1)
                        dve.reg_mov(wn_dve, 1)

                    def leave(g, par):
                        dve.wait_ge(s_part0, g + (past + 1))
                        nv.tensor_tensor(rest[:, :, 0:cols], prod[:, par, :, 0:cols], parts[:, par, :, 0, 0:cols], ALU.subtract).then_inc(s_rest, 1)

                    def part2(g, par):
                        dve.wait_ge(s_part1, g + (past + 1))
                        nv.tensor_tensor(parts[:, par, :, 2, 0:cols], rest[:, :, 0:cols], parts[:, par, :, 1, 0:cols], ALU.subtract).then_inc(s_part2, 1)

                    leave(0, 0)
                    with dve.Fori(0, TURNS) as i:
                        spans = load_ranges(dve, i)
                        for j in range(GB):
                            g = i * GB + j
                            part2(g, j % 2)
                            if first:
                                dve.wait_ge(s_bcast[j % 2], i * (16 * GB) + 32 * (j // 2 + 1))
                                dve.sem_inc(s_seen, 1)
                            with dve.Fori(*spans[j]) as k:
                                win = dve.snap(wn_dve)
                                nv.tensor_tensor(onehot[:, :, :], iota[:, ds(k * P, P)].unsqueeze(1).to_broadcast([P, G, P]),
                                                 dstf[:, ds(i * U + j * G, G)].unsqueeze(2).to_broadcast([P, G, P]),
                                                 ALU.is_equal).then_inc(s_hot, 1)
                                if first:
                                    dve.wait_ge(s_exp, win)
                                    dve.sem_inc(s_seen, 1)
                                    nv.tensor_scalar(onet[:, :], drow[:, j % 2, :], node[:, ds(k, 1)], None, ALU.is_equal).then_inc(s_onet, 1)
                                    dve.wait_ge(s_pen, win)
                                    dve.wait_ge(s_maxed, win)
                                    dve.sem_inc(s_seen, 1)
                                    nv.tensor_tensor_reduce(out=junk, in0=lrow[:, j % 2, :], in1=pen[:, :], scale=1.0, scalar=-BIG,
                                                            op0=ALU.subtract, op1=ALU.max, accum_out=wmax[:, :]).then_inc(s_wmax, 1)
                                dve.wait_ge(s_added, win)
                                dve.wait_ge(s_mm, win)
                                nv.tensor_tensor(acc[:, ds(k, 1), 0:cols].rearrange("p b c -> p (b c)"), acc[:, ds(k, 1), 0:cols].rearrange("p b c -> p (b c)"),
                                                 psum_acc[:, 0:cols], ALU.add).then_inc(s_added, 1)
                                if first:
                                    dve.wait_ge(s_wmax, win)
                                    nv.tensor_tensor(segmax[:, ds(k, 1)], segmax[:, ds(k, 1)], wmax[:, :],
                                                     ALU.max).then_inc(s_maxed, 1)
                                dve.reg_add(wn_dve, wn_dve, 1)
                            leave(g + 1, (j + 1) % 2)
                            if first:
                                pq = psum_exp[j % 2][:, 0:G * GE].rearrange("p (g c) -> p g c", c=GE)
                                dve.wait_ge(s_closed, g + 1)
                                for u in range(G):
                                    last = nv.tensor_tensor_reduce(out=dots[:, u, :], in0=rows[:, j % RING * G + u, C:C0], in1=pq[:, u, :], scale=1.0,
                                                                   scalar=0.0, op0=ALU.mult, op1=ALU.add,
                                                                   accum_out=adaptg[:, u:u + 1])
                                last.then_inc(s_free, 1)

                @block.tensor
                def _(pe):
                    if first:
                        pe.sem_inc(s_mlp1, 2)
                        pe.reg_mov(wn_pe, 1)
                    with pe.Fori(0, TURNS) as i:
                        spans = load_ranges(pe, i)
                        for j in range(GB):
                            g = i * GB + j
                            if first:
                                pe.wait_ge(s_attr[j % 2], i * (8 * GB) + 16 * (j // 2 + 1))
                                pe.sem_inc(s_seen, 1)
                                pe.wait_ge(s_hid, g + 1)
                                pe.sem_inc(s_seen, 1)
                                nc.tensor.matmul(psum_mlp[j % 2][0:C, :], w1s[:, :], attr[j % 2], start=True, stop=True).then_inc(s_mlp1, 1)
                                pe.wait_ge(s_free, g + (RING - 1))
                                nc.tensor.matmul(psum_exp[j % 2][:, 0:G * GE], zeros[0:1, 0:P], zeros[0:1, 0:G * GE],
                                                 start=True, stop=False)
                            pe.wait_ge(s_part2, g + (passed + 1))
                            pe.sem_inc(s_seen, 1)
                            with pe.Fori(*spans[j]) as k:
                                win = pe.snap(wn_pe)
                                pe.wait_ge(s_hot, win)
                                for u in range(G):
                                    for q in range(PARTS):
                                        last = nc.tensor.matmul(psum_acc[:, 0:cols], onehot[:, u, :], parts[:, j % 2, u, q, 0:cols],
                                                                start=(u == 0 and q == 0), stop=(u == G - 1 and q == PARTS - 1))
                                last.then_inc(s_mm, 1)
                                if first:
                                    pe.wait_ge(s_onet, win)
                                    for u in range(G):
                                        for q in range(PARTS):
                                            last = nc.tensor.matmul(psum_exp[j % 2][:, u * GE:(u + 1) * GE], onet[:, u * P:(u + 1) * P],
                                                                    embq[:, ds(k, 1), q, :].rearrange("p b c -> p (b c)"),
                                                                    start=False, stop=False)
                                    last.then_inc(s_exp, 1)
                                pe.reg_add(wn_pe, wn_pe, 1)
                            if first:
                                nc.tensor.matmul(psum_exp[j % 2][:, 0:G * GE], zeros[0:1, 0:P], zeros[0:1, 0:G * GE],
                                                 start=False, stop=True).then_inc(s_closed, 1)

        spmm_pass(0, "l0", table0, C, w, True)

        s_var1 = sem("s_var1"); s_std1 = sem("s_std1")
        with nc.Block() as block:
            @block.vector
            def _(dve):
                link = chain(dve, "s_epi0_chain")
                link(nv.tensor_tensor(adapt[:, G:], adapt[:, G:], cw[:, :], ALU.mult))
                link(nv.memset(table[:, NB:NBW, :, :], 0.0))
                link(nv.tensor_tensor(nodes[:, :, :], nodes[:, :, :], acc[:, 0:NB, 0:C], ALU.add))
                layernorm_relu(link, nv, s_var1, s_std1, 0, nodes[:, :, :], h[:, :, :])
                hm = scratch[:, 0:NB * C].rearrange("p (b c) -> p b c", c=C)
                link(nv.tensor_tensor(hm, h[:, :, :], multc[:, :].unsqueeze(2).to_broadcast([P, NB, C]), ALU.mult))
                left = acc[:, 0:NB, 0:C]
                split(link, table[:, 0:NB, :, 0:C], hm, left)
                split(link, table[:, 0:NB, :, C:C + 1], multc[:, :].unsqueeze(2), left[:, :, 0:1])
                split(link, table[:, 0:NB, :, C + 1:CT], segmax[:, 0:NB].unsqueeze(2), left[:, :, 0:1])

            @block.scalar
            def _(act):
                std(act, s_var1, s_std1, 0)

        s_in = [sem(f"l1_in{r}") for r in range(2)]
        s_hidin = [sem(f"l1_hidin{r}") for r in range(2)]
        s_same = sem("l1_same"); s_dup = sem("l1_dup"); s_dmp = sem("l1_dmp"); s_idx1 = sem("l1_idx")
        s_onet1 = sem("l1_onet")
        s_closed1 = sem("l1_closed")
        s_exp1 = sem("l1_exp")
        s_mlp = sem("l1_mlp")
        s_gate = sem("l1_gate")
        s_msg = sem("l1_msg")
        s_p0 = sem("l1_p0"); s_r = sem("l1_r"); s_p1 = sem("l1_p1"); s_p2 = sem("l1_p2")
        s_comb = sem("l1_comb")
        s_out = sem("l1_out")
        s_scat = [sem(f"l1_scat{c}") for c in range(K)]
        s_landed = sem("l1_landed")
        wn1_dve = nc.vector.alloc_register("l1_dve_window")
        wn1_pe = nc.tensor.alloc_register("l1_pe_window")
        with nc.Block() as block:
            @block.sync
            def _(sp):
                with sp.Fori(0, TURNS) as i:
                    for j in range(GB):
                        g = i * GB + j
                        sp.wait_ge(s_mlp, g + 1)
                        sp.sem_inc(s_seen, 1)
                        sp.dma_start(hid[0:C, j % 2, :], hid_dram[:, ds(g * GW, GW)]).then_inc(s_hidin[j % 2], 16)
                        sp.wait_ge(s_msg, g + 1)
                        sp.sem_inc(s_seen, 1)
                        sp.dma_start(drow[:, j % 2, :], rows16_dram[0, ds(g, 1), :].squeeze(0).partition_broadcast(P)).then_inc(s_in[j % 2], 16)
                        sp.dma_start(srcrow[:, j % 2, :], rows16_dram[1, ds(g, 1), :].squeeze(0).partition_broadcast(P)).then_inc(s_in[j % 2], 16)

                sp.wait_ge(s_mlp, NG + 1)
                sp.sem_inc(s_hidin[NG % 2], 16)

            @block.vector
            def _(dve):
                dve.sem_inc(s_msg, 2)
                dve.sem_inc(s_exp1, 1)
                dve.reg_mov(wn1_dve, 1)

                def leave(g, par):
                    dve.wait_ge(s_p0, g + 1)
                    nv.tensor_tensor(rest[:, :, :], prod[:, par, :, :], parts[:, par, :, 0, :], ALU.subtract).then_inc(s_r, 1)

                def part2(g, par):
                    dve.wait_ge(s_p1, g + 1)
                    nv.tensor_tensor(parts[:, par, :, 2, :], rest[:, :, :], parts[:, par, :, 1, :], ALU.subtract).then_inc(s_p2, 1)

                def turn(i, peeled):
                    spans = load_ranges(dve, i)
                    for j in range(GB):
                        g = i * GB + j
                        behind = j > 0 or not peeled
                        dve.wait_ge(s_in[j % 2], i * (16 * GB) + 32 * (j // 2 + 1))
                        dve.sem_inc(s_seen, 1)
                        with dve.Fori(*spans[j]) as k:
                            win = dve.snap(wn1_dve)
                            dve.wait_ge(s_exp1, win)
                            dve.sem_inc(s_seen, 1)
                            nv.tensor_scalar(onet[:, :], drow[:, j % 2, :], node[:, ds(k, 1)], None, ALU.is_equal).then_inc(s_onet1, 1)
                            dve.reg_add(wn1_dve, wn1_dve, 1)
                        if j >= 2 or not peeled:
                            dve.wait_ge(s_comb, g - 1)
                            dve.sem_inc(s_seen, 1)
                        for u in range(G):
                            nv.tensor_scalar(same[:, j % 2, u, :], srcrow[:, j % 2, u * P:(u + 1) * P],
                                             srow[:, ds(i * U + (j * G + u), 1)], None, ALU.is_equal).then_inc(s_same, 1)
                        if behind:
                            leave(g - 1, (j - 1) % 2)
                        dve.wait_ge(s_same, g * G + G)
                        dve.sem_inc(s_seen, 1)
                        for u in range(G):
                            nv.tensor_tensor_reduce(out=onehot[:, u, 0:P], in0=same[:, j % 2, u, :], in1=lower[:, :], scale=1.0, scalar=0.0,
                                                    op0=ALU.mult, op1=ALU.max, accum_out=dup[:, u:u + 1]).then_inc(s_dup, 1)
                        if behind:
                            part2(g - 1, (j - 1) % 2)
                        dve.wait_ge(s_dup, g * G + G)
                        nv.scalar_tensor_tensor(out=dmp[:, :], in0=srow[:, ds(i * U + j * G, G)], scalar=trash[:, 0:1],
                                                in1=dup[:, :], op0=ALU.subtract, op1=ALU.mult).then_inc(s_dmp, 1)
                        dve.wait_ge(s_closed1, g + 1)
                        dve.sem_inc(s_seen, 1)
                        ph = psum_exp[j % 2][:, 0:G * CT].rearrange("p (g c) -> p g c", c=CT)
                        nv.tensor_tensor(lg[:, ds(i * U + j * G, G)], lg[:, ds(i * U + j * G, G)], ph[:, :, C + 1], ALU.subtract)
                        dve.wait_ge(s_gate, g + 3)
                        nv.tensor_tensor(prod[:, j % 2, :, :], gate[:, j % 2, :, :], ph[:, :, 0:CS], ALU.mult).then_inc(s_msg, 1)
                        dve.wait_ge(s_dmp, g + 1)
                        dve.wait_ge(s_landed, g + (RING - 1))
                        nv.tensor_tensor(idx[:, j % RING * G:(j % RING + 1) * G], srow[:, ds(i * U + j * G, G)], dmp[:, :],
                                         ALU.subtract).then_inc(s_idx1, 1)

                turn(0, True)
                with dve.Fori(1, TURNS) as i:
                    turn(i, False)
                leave(NG - 1, (NG - 1) % 2)
                part2(NG - 1, (NG - 1) % 2)

            @block.tensor
            def _(pe):
                pe.sem_inc(s_mlp, 2)
                pe.reg_mov(wn1_pe, 1)

                def second_layer(i, j):
                    pe.wait_ge(s_hidin[j % 2], i * (8 * GB) + 16 * (j // 2 + 1))
                    pe.sem_inc(s_seen, 1)
                    pe.wait_ge(s_gate, i * GB + (j + 1))
                    pe.sem_inc(s_seen, 1)
                    for u in range(G):
                        last = nc.tensor.matmul(psum_mlp[j % 2][:, u * C:(u + 1) * C], hid[:, j % 2, u * P:(u + 1) * P], w2s[:, :],
                                                start=True, stop=True)
                    last.then_inc(s_mlp, 1)

                def combine(g, par):
                    pe.wait_ge(s_p2, g + 1)
                    pe.sem_inc(s_seen, 1)
                    pe.wait_ge(s_out, g + 1)
                    for u in range(G):
                        for q in range(PARTS):
                            last = nc.tensor.matmul(psum_comb[par][:, u * CS:(u + 1) * CS], same[:, par, u, :], parts[:, par, u, q, :],
                                                    start=(q == 0), stop=(q == PARTS - 1))
                    last.then_inc(s_comb, 1)

                def turn(i, peeled):
                    spans = load_ranges(pe, i)
                    for j in range(GB):
                        g = i * GB + j
                        pe.wait_ge(s_msg, g + 1)
                        nc.tensor.matmul(psum_exp[j % 2][:, 0:G * CT], zeros[0:1, 0:P], zeros[0:1, 0:G * CT], start=True, stop=False)
                        with pe.Fori(*spans[j]) as k:
                            win = pe.snap(wn1_pe)
                            pe.wait_ge(s_onet1, win)
                            for u in range(G):
                                for q in range(PARTS):
                                    last = nc.tensor.matmul(psum_exp[j % 2][:, u * CT:(u + 1) * CT], onet[:, u * P:(u + 1) * P],
                                                            table[:, ds(k, 1), q, :].rearrange("p b c -> p (b c)"),
                                                            start=False, stop=False)
                            last.then_inc(s_exp1, 1)
                            pe.reg_add(wn1_pe, wn1_pe, 1)
                        nc.tensor.matmul(psum_exp[j % 2][:, 0:G * CT], zeros[0:1, 0:P], zeros[0:1, 0:G * CT], start=False,
                                         stop=True).then_inc(s_closed1, 1)
                        second_layer(i, j + 1)
                        if j > 0 or not peeled:
                            combine(g - 1, (j - 1) % 2)

                second_layer(0, 0)
                turn(0, True)
                with pe.Fori(1, TURNS) as i:
                    turn(i, False)
                combine(NG - 1, (NG - 1) % 2)

            @block.scalar
            def _(act):
                act.sem_inc(s_out, 2)
                act.sem_inc(s_gate, 2)

                def part0(g, par):
                    act.wait_ge(s_msg, g + 3)
                    act.sem_inc(s_seen, 1)
                    nc.scalar.copy(parts[:, par, :, 0, :], prod[:, par, :, :]).then_inc(s_p0, 1)

                def part1(g, par):
                    act.wait_ge(s_r, g + 1)
                    act.sem_inc(s_seen, 1)
                    nc.scalar.copy(parts[:, par, :, 1, :], rest[:, :, :]).then_inc(s_p1, 1)

                def hand_over(g, slot):
                    act.wait_ge(s_comb, g + 1)
                    act.sem_inc(s_seen, 1)
                    act.wait_ge(s_landed, g + (RING - 1))
                    nc.scalar.activation(rows[:, slot * G:(slot + 1) * G, 0:CS],
                                         psum_comb[slot % 2][:, 0:G * CS].rearrange("p (g c) -> p g c", c=CS), ACT.Copy).then_inc(s_out, 1)

                def turn(i, peeled):
                    for j in range(GB):
                        g = i * GB + j
                        act.wait_ge(s_mlp, g + 3)
                        act.sem_inc(s_seen, 1)
                        act.wait_ge(s_msg, g + 1)
                        act.sem_inc(s_seen, 1)
                        for u in range(G):
                            t = i * U + (j * G + u)
                            last = nc.scalar.activation(gate[:, j % 2, u, 0:C], psum_mlp[j % 2][:, u * C:(u + 1) * C], ACT.Identity,
                                                        scale=cw[:, ds(t, 1)], bias=adapt[:, ds(t + G, 1)])
                        last.then_inc(s_gate, 1)
                        if j > 0 or not peeled:
                            part1(g - 1, (j - 1) % 2)
                        part0(g, j % 2)
                        if j > 0 or not peeled:
                            hand_over(g - 1, (j - 1) % RING)

                turn(0, True)
                with act.Fori(1, TURNS) as i:
                    turn(i, False)
                part1(NG - 1, (NG - 1) % 2)
                hand_over(NG - 1, RING - 1)

            @block.gpsimd
            def _(pool):
                pool.sem_inc(s_landed, RING)

                def turn(i, peeled):
                    for j in range(GB):
                        g = i * GB + j
                        pool.wait_ge(s_idx1, g + 1)
                        pool.sem_inc(s_seen, 1)
                        pool.wait_ge(s_out, g + 3)
                        pool.sem_inc(s_seen, 1)
                        for u in range(j * G, (j + 1) * G):
                            c, slot = u % K, u % (RING * G)
                            if u >= K or not peeled:
                                pool.wait_ge(s_scat[c], i * (16 * U // K) + 16 * (u // K))
                                pool.sem_inc(s_seen, 1)
                            pool.indirect_dma_start(out=sums[c], out_offset=bass.IndirectOffsetOnAxis(ap=idx[:, slot:slot + 1], axis=0),
                                                    in_=rows[:, slot, 0:CS], in_offset=None, compute_op=ALU.add).then_inc(s_scat[c], 16)
                        pool.sem_inc(s_landed, 1)

                turn(0, True)
                with pool.Fori(1, TURNS) as i:
                    turn(i, False)
                for c in range(K):
                    pool.wait_ge(s_scat[c], 16 * T // K)

        s_var2 = sem("s_var2"); s_std2 = sem("s_std2"); s_exped = sem("s_exped")
        s_sum = [sem(f"s_sum{r}") for r in range(3)]
        s_used = sem("s_used"); s_t2 = sem("s_t2"); s_t2out = sem("s_t2out")
        n49 = NB * CS
        copies = [tbl_flat[:, 0:n49], scratch[:, 0:n49]]
        flat_acc = acc_flat[:, 0:n49]
        t2 = tbl_flat[:, 0:n49].rearrange("p (b c) -> p b c", c=CS)
        with nc.Block() as block:
            @block.sync
            def _(sp):
                sp.dma_start(flat_acc, sums[0][0:NPAD, :].rearrange("(p b) c -> p (b c)", p=P)).then_inc(s_sum[2], 16)
                for c in range(1, K):
                    if c >= 3:
                        sp.wait_ge(s_used, c - 2)
                    sp.dma_start(copies[c % 2], sums[c][0:NPAD, :].rearrange("(p b) c -> p (b c)", p=P)).then_inc(s_sum[c % 2], 16)
                table_out(sp, s_t2, s_t2out, table2, tbl_flat[:, 0:n49])

            @block.vector
            def _(dve):
                link = chain(dve, "s_epi1_chain")
                link(nv.tensor_tensor(nodes[:, :, :], nodes[:, :, :], betab[:, :].unsqueeze(1).to_broadcast([P, NB, C]), ALU.add))
                dve.wait_ge(s_sum[2], 16)
                for c in range(1, K):
                    dve.wait_ge(s_sum[c % 2], 16 * ((c + 1) // 2))
                    nv.tensor_tensor(flat_acc, flat_acc, copies[c % 2], ALU.add).then_inc(s_used, 1)
                    dve.wait_ge(s_used, c)
                tot = stat[:, 0, :]
                link(nv.tensor_scalar(tot, acc[:, 0:NB, C], 1e-8, None, ALU.max))
                link(nv.reciprocal(stat[:, 1, :], tot))
                link(nv.tensor_tensor(acc[:, 0:NB, 0:C], acc[:, 0:NB, 0:C], stat[:, 1, :].unsqueeze(2).to_broadcast([P, NB, C]), ALU.mult))
                link(nv.tensor_tensor(h[:, :, :], h[:, :, :], acc[:, 0:NB, 0:C], ALU.add))
                link(nv.memset(t2[:, :, C:CS], 1.0))
                layernorm_relu(link, nv, s_var2, s_std2, 0, h[:, :, :], acc[:, 0:NB, 0:C], gammab[:, :])
                link(nv.tensor_tensor(nodes[:, :, :], nodes[:, :, :], acc[:, 0:NB, 0:C], ALU.add))
                layernorm_relu(link, nv, s_var2, s_std2, 1, nodes[:, :, :], t2[:, :, 0:C], made=s_t2)

            @block.scalar
            def _(act):
                std(act, s_var2, s_std2, 0)
                std(act, s_var2, s_std2, 1)
                nc.scalar.activation(lg[:, :], lg[:, :], ACT.Exp).then_inc(s_exped, 1)

        spmm_pass(1, "l2", table2, CS, lg, False)

        s_var3 = sem("s_var3"); s_std3 = sem("s_std3"); s_neg = sem("s_neg"); s_elu = sem("s_elu")
        s_h3 = sem("s_h3"); s_h3out = sem("s_h3out")
        e3 = scratch[:, 0:NB * C].rearrange("p (b c) -> p b c", c=C)
        with nc.Block() as block:
            @block.sync
            def _(sp):
                table_out(sp, s_h3, s_h3out, table3[0], h_flat)

            @block.vector
            def _(dve):
                link = chain(dve, "s_epi2_chain")
                a3 = acc[:, 0:NB, 0:C]
                link(nv.tensor_scalar(stat[:, 0, :], acc[:, 0:NB, C], 1e-30, None, ALU.max))
                link(nv.reciprocal(stat[:, 1, :], stat[:, 0, :]))
                link(nv.tensor_tensor(a3, a3, stat[:, 1, :].unsqueeze(2).to_broadcast([P, NB, C]), ALU.mult))
                nv.tensor_scalar(e3, a3, 0.0, None, ALU.min).then_inc(s_neg, 1)
                link(nv.tensor_scalar(a3, a3, 0.0, -1.0, ALU.max, ALU.add))
                link(nv.tensor_tensor(nodes[:, :, :], nodes[:, :, :], a3, ALU.add))
                dve.wait_ge(s_elu, 1)
                link(nv.tensor_tensor(nodes[:, :, :], nodes[:, :, :], e3, ALU.add))
                layernorm_relu(link, nv, s_var3, s_std3, 0, nodes[:, :, :], h[:, :, :], made=s_h3)

            @block.scalar
            def _(act):
                act.wait_ge(s_neg, 1)
                nc.scalar.activation(scratch[:, 0:NB * C], scratch[:, 0:NB * C], ACT.Exp).then_inc(s_elu, 1)
                std(act, s_var3, s_std3, 0)

        spmm_pass(2, "l3a", table3[0], C, w, False)
        s_y1 = sem("s_y1"); s_y1out = sem("s_y1out")
        third = 1.0 / (LAYERS + 1)
        with nc.Block() as block:
            @block.sync
            def _(sp):
                table_out(sp, s_y1, s_y1out, table3[1], scratch[:, 0:NB * C])

            @block.vector
            def _(dve):
                link = chain(dve, "s_epi3_chain")
                for b in range(0, NB, NB // 2):
                    nv.tensor_copy(e3[:, b:b + NB // 2, :], acc[:, b:b + NB // 2, 0:C]).then_inc(s_y1, 1)
                link(nv.tensor_tensor(h[:, :, :], h[:, :, :], acc[:, 0:NB, 0:C], ALU.add))
                link(nv.scalar_tensor_tensor(out=nodes[:, :, :], in0=h[:, :, :], scalar=third, in1=nodes[:, :, :], op0=ALU.mult, op1=ALU.add))

        spmm_pass(3, "l3b", table3[1], C, w, False)
        s_res = sem("s_res"); s_resout = sem("s_resout")
        with nc.Block() as block:
            @block.vector
            def _(dve):
                nv.scalar_tensor_tensor(out=nodes[:, :, :], in0=acc[:, 0:NB, 0:C], scalar=third, in1=nodes[:, :, :],
                                        op0=ALU.mult, op1=ALU.add).then_inc(s_res, 1)

            @block.sync
            def _(sp):
                sp.wait_ge(s_res, 1)
                sp.dma_start(out, nodes[:, :, :].rearrange("p b c -> p (b c)")).then_inc(s_resout, 16)
                sp.wait_ge(s_resout, 16)


def kernel(x, src, dst, edge_attr_40, edge_weight, edge_weight1, node_type_119, node_vec, L1_gnn_W1, L1_gnn_b1,
           L1_gnn_W2, L1_gnn_b2, L1_gnn_emb, L1_gnn_adaptW, L1_gnn_gamma, L1_gnn_beta):
    import numpy as np
    import concourse.bacc as bacc
    from concourse.bass_utils import run_bass_kernel_spmd

    def padded(a, n, fill=0):
        a = np.asarray(a)
        return np.concatenate([a, np.full((n - a.shape[0],) + a.shape[1:], fill, a.dtype)])

    def node_major(a):
        a = padded(a, NPAD)
        a = a.reshape(NB, P, -1).transpose(1, 0, 2)
        return a.reshape(P, -1)

    ne = T * P
    last = NPAD - 1
    s, d = padded(src, ne, last), padded(dst, ne, last)
    ew, lgt = padded(edge_weight, ne), padded(np.asarray(edge_weight1)[:, 0], ne)
    arrays = {
        "x": node_major(x),
        "dst_cols": d.reshape(T, P).T, "src_cols": s.reshape(T, P).T,
        "dst_rows": d.reshape(NG, GW), "src_rows": s.reshape(NG, GW),
        "w_cols": ew.reshape(T, P).T, "logit_cols": lgt.reshape(T, P).T, "logit_rows": lgt.reshape(NG, GW),
        "attr_t": padded(edge_attr_40, ne).T,
        "type_row": padded(node_type_119, NPAD).reshape(1, NPAD),
        "mult": node_major(node_vec),
        "w1_t": np.asarray(L1_gnn_W1).T, "b1": np.asarray(L1_gnn_b1).reshape(C, 1),
        "w2e": np.concatenate([np.asarray(L1_gnn_W2).T, np.asarray(L1_gnn_b2).reshape(1, C)]),
        "emb": np.asarray(L1_gnn_emb), "emb_t": np.asarray(L1_gnn_emb).T, "adapt_t": np.asarray(L1_gnn_adaptW).T,
        "gamma": np.asarray(L1_gnn_gamma), "beta": np.asarray(L1_gnn_beta),
    }
    arrays = {f"in_{k}": np.ascontiguousarray(v) for k, v in arrays.items()}
    nc = bacc.Bacc("TRN2", target_bir_lowering=False, num_devices=1)
    args = [nc.dram_tensor(k, v.shape, mybir.dt.from_np(v.dtype), kind="ExternalInput").ap() for k, v in arrays.items()]
    out = nc.dram_tensor("out", (P, NB * C), mybir.dt.float32, kind="ExternalOutput").ap()
    gnn_kernel(nc, *args, out)
    r = run_bass_kernel_spmd(nc, [arrays], core_ids=[0])
    y = np.asarray(r.results[0]["out"]).reshape(P, NB, C).transpose(1, 0, 2).reshape(NPAD, C)
    return np.ascontiguousarray(y[:N])
```
